# Optimizing a Trainium2 kernel written in Bass

```python
import numpy as np
import jax
import jax.numpy as jnp

def _softmax(x, axis=-1):
    return jax.nn.softmax(x, axis=axis)

def _gelu(x):
    return jax.nn.gelu(x, approximate=True)

def _silu(x):
    return jax.nn.silu(x)

def _sigmoid(x):
    return jax.nn.sigmoid(x)

def _layernorm(x, axis=-1, eps=1e-05):
    m = jnp.mean(x, axis=axis, keepdims=True)
    v = jnp.var(x, axis=axis, keepdims=True)
    return (x - m) / jnp.sqrt(v + eps)

def _scatter_add(tgt, idx, src, axis=0):
    return tgt.at[idx].add(src)

def _segment_sum(src, seg, n):
    return jax.ops.segment_sum(src, seg, n)
kernel_name = 'mk_gnn_preln_d2_gnn_r32_623a99'

def setup_inputs(seed: int=0):
    np.random.seed(seed)
    _w = jnp.asarray

    def _rec_inputs():
        import jax
        import jax.numpy as jnp
        _gk = jax.random.key(seed)
        x = -0.000202 + 1 * jax.random.normal(jax.random.fold_in(_gk, 1), (3125, 64), jnp.float32)
        _s = jax.random.randint(jax.random.fold_in(_gk, 2), (50000,), 0, 3125, jnp.int32)
        _d = jax.random.randint(jax.random.fold_in(_gk, 3), (50000,), 0, 3125, jnp.int32)
        _loop = jnp.arange(3125, dtype=jnp.int32)
        src = jnp.concatenate([_s, _d, _loop])
        dst = jnp.concatenate([_d, _s, _loop])
        _o = jnp.argsort(dst, stable=True)
        src = src[_o]
        dst = dst[_o]
        edge_attr_64 = -8.16379e-05 + 0.999858 * jax.random.normal(jax.random.fold_in(_gk, 12), (103125, 64), jnp.float32)
        edge_weight = jax.random.uniform(jax.random.fold_in(_gk, 13), (103125,), jnp.float32, 0.0, 0.0625)
        return (x, src, dst, edge_attr_64, edge_weight)
    x, src, dst, edge_attr_64, edge_weight = _rec_inputs()

    def _L0_gnn_setup():
        import jax, jax.numpy as jnp
        import numpy as np
        N = 3125
        E = 50000
        DN = 64
        DE = 64

        def _w(k, shape):
            fan_in = shape[0]
            return jax.random.normal(k, shape, dtype=jnp.float32) / np.sqrt(fan_in)
        key = jax.random.key(seed)
        ks = jax.random.split(key, 12)
        x = jax.random.normal(ks[0], (N, DN), dtype=jnp.float32)
        e = jax.random.normal(ks[1], (E, DE), dtype=jnp.float32)
        senders = jax.random.randint(ks[2], (E,), 0, N)
        receivers = jax.random.randint(ks[3], (E,), 0, N)
        return {'x': x, 'e': e, 'senders': senders, 'receivers': receivers, 'We1': _w(ks[4], (DE + 2 * DN, DE)), 'be1': jnp.zeros((DE,), jnp.float32), 'We2': _w(ks[5], (DE, DE)), 'be2': jnp.zeros((DE,), jnp.float32), 'We3': _w(ks[6], (DE, DE)), 'be3': jnp.zeros((DE,), jnp.float32), 'Wn1': _w(ks[7], (DN + DE, DN)), 'bn1': jnp.zeros((DN,), jnp.float32), 'Wn2': _w(ks[8], (DN, DN)), 'bn2': jnp.zeros((DN,), jnp.float32), 'Wn3': _w(ks[9], (DN, DN)), 'bn3': jnp.zeros((DN,), jnp.float32)}
    _L0_gnn_all = _L0_gnn_setup()
    _L0_gnn_in = {k: v for k, v in _L0_gnn_all.items() if k in ('We1', 'be1', 'We2', 'be2', 'We3', 'be3', 'Wn1', 'bn1', 'Wn2', 'bn2', 'Wn3', 'bn3')}
    del _L0_gnn_all

    def _L1_gnn_setup():
        import jax, jax.numpy as jnp
        import numpy as np
        V = 3125
        C = 64
        D = 64
        W = 8
        DEG = 16
        E = V * DEG
        key = jax.random.key(seed)
        k = jax.random.split(key, 6)
        data = jax.random.normal(k[0], (V, C), dtype=jnp.float32)
        edge_src = jnp.repeat(jnp.arange(V, dtype=jnp.int32), DEG)
        edge_dst = jax.random.randint(k[1], (E,), 0, V, dtype=jnp.int32)
        edge_vals = jnp.full((E,), 1.0 / DEG, dtype=jnp.float32)
        var_u = 0.1 * jax.random.normal(k[2], (C, W), dtype=jnp.float32)
        var_c = 0.1 * jax.random.normal(k[3], (W,), dtype=jnp.float32)
        var_w = 0.1 * jax.random.normal(k[4], (W, C, D), dtype=jnp.float32)
        var_b = 0.1 * jax.random.normal(k[5], (D,), dtype=jnp.float32)
        return {'data': data, 'edge_src': edge_src, 'edge_dst': edge_dst, 'edge_vals': edge_vals, 'var_u': var_u, 'var_c': var_c, 'var_w': var_w, 'var_b': var_b}
    _L1_gnn_all = _L1_gnn_setup()
    _L1_gnn_in = {k: v for k, v in _L1_gnn_all.items() if k in ('var_u', 'var_c', 'var_w', 'var_b')}
    del _L1_gnn_all
    return {'x': x, 'src': src, 'dst': dst, 'edge_attr_64': edge_attr_64, 'edge_weight': edge_weight, 'L0_gnn_We1': _L0_gnn_in['We1'], 'L0_gnn_be1': _L0_gnn_in['be1'], 'L0_gnn_We2': _L0_gnn_in['We2'], 'L0_gnn_be2': _L0_gnn_in['be2'], 'L0_gnn_We3': _L0_gnn_in['We3'], 'L0_gnn_be3': _L0_gnn_in['be3'], 'L0_gnn_Wn1': _L0_gnn_in['Wn1'], 'L0_gnn_bn1': _L0_gnn_in['bn1'], 'L0_gnn_Wn2': _L0_gnn_in['Wn2'], 'L0_gnn_bn2': _L0_gnn_in['bn2'], 'L0_gnn_Wn3': _L0_gnn_in['Wn3'], 'L0_gnn_bn3': _L0_gnn_in['bn3'], 'L1_gnn_var_u': _L1_gnn_in['var_u'], 'L1_gnn_var_c': _L1_gnn_in['var_c'], 'L1_gnn_var_w': _L1_gnn_in['var_w'], 'L1_gnn_var_b': _L1_gnn_in['var_b']}

def reference(x, src, dst, edge_attr_64, edge_weight, L0_gnn_We1, L0_gnn_be1, L0_gnn_We2, L0_gnn_be2, L0_gnn_We3, L0_gnn_be3, L0_gnn_Wn1, L0_gnn_bn1, L0_gnn_Wn2, L0_gnn_bn2, L0_gnn_Wn3, L0_gnn_bn3, L1_gnn_var_u, L1_gnn_var_c, L1_gnn_var_w, L1_gnn_var_b):
    import jax
    import jax.numpy as jnp

    def _L0_gnn_ref(x, e, senders, receivers, We1, be1, We2, be2, We3, be3, Wn1, bn1, Wn2, bn2, Wn3, bn3):
        import jax, jax.numpy as jnp
        import numpy as np
        N = 3125
        E = 50000
        DN = 64
        DE = 64

        def _w(k, shape):
            fan_in = shape[0]
            return jax.random.normal(k, shape, dtype=jnp.float32) / np.sqrt(fan_in)
        h = jnp.concatenate([e, x[senders], x[receivers]], axis=-1)
        h = jax.nn.relu(h @ We1 + be1)
        h = jax.nn.relu(h @ We2 + be2)
        e_new = h @ We3 + be3
        agg = jax.ops.segment_sum(e_new, receivers, num_segments=N)
        g = jnp.concatenate([x, agg], axis=-1)
        g = jax.nn.relu(g @ Wn1 + bn1)
        g = jax.nn.relu(g @ Wn2 + bn2)
        x_new = g @ Wn3 + bn3
        return x_new

    def _L1_gnn_ref(data, edge_src, edge_dst, edge_vals, var_u, var_c, var_w, var_b):
        import jax, jax.numpy as jnp
        import numpy as np
        V = 3125
        C = 64
        D = 64
        W = 8
        DEG = 16
        E = V * DEG
        num_v = data.shape[0]
        x_u = data @ var_u
        x_v = data @ -var_u
        logits = x_u[edge_src] + x_v[edge_dst] + var_c
        q = jax.nn.softmax(logits, axis=-1)
        x_sep = data[edge_dst] * edge_vals[:, None]
        y = jnp.zeros((num_v, var_w.shape[-1]), dtype=data.dtype)
        for m in range(var_c.shape[0]):
            agg = jax.ops.segment_sum(q[:, m:m + 1] * x_sep, edge_src, num_segments=num_v)
            y = y + agg @ var_w[m]
        return y + var_b
    h = jnp.maximum(_layernorm(x, axis=-1), 0.0)
    x = x + _L0_gnn_ref(h, edge_attr_64, src, dst, L0_gnn_We1, L0_gnn_be1, L0_gnn_We2, L0_gnn_be2, L0_gnn_We3, L0_gnn_be3, L0_gnn_Wn1, L0_gnn_bn1, L0_gnn_Wn2, L0_gnn_bn2, L0_gnn_Wn3, L0_gnn_bn3)
    h = jnp.maximum(_layernorm(x, axis=-1), 0.0)
    x = x + _L1_gnn_ref(h, src, dst, edge_weight, L1_gnn_var_u, L1_gnn_var_c, L1_gnn_var_w, L1_gnn_var_b)
    return x

_drawn_inputs = setup_inputs


def setup_inputs(seed=0):
    import zlib

    import numpy as np

    out = dict(_drawn_inputs(seed))
    spreads = {'L0_gnn_be1': (0.0, 0.1),
     'L0_gnn_be2': (0.0, 0.1),
     'L0_gnn_be3': (0.0, 0.1),
     'L0_gnn_bn1': (0.0, 0.683),
     'L0_gnn_bn2': (0.0, 0.678),
     'L0_gnn_bn3': (0.0, 0.378)}
    factors = {'edge_weight': 8.0, 'L1_gnn_var_u': 8.0, 'L1_gnn_var_c': 8.0, 'L1_gnn_var_b': 2.732}
    for name, (base, spread) in spreads.items():
        noise = np.random.default_rng([zlib.crc32(name.encode()), seed]).standard_normal(out[name].shape)
        drawn = base * np.exp(spread * noise) if base else spread * noise
        out[name] = jnp.asarray(drawn.astype(out[name].dtype))
    for name, factor in factors.items():
        out[name] = (out[name] * factor).astype(out[name].dtype)
    return out
```

```python
from contextlib import ExitStack

import concourse.bass as bass
from concourse import mybir

F32 = mybir.dt.float32
I32 = mybir.dt.int32
ALU = mybir.AluOpType
ACT = mybir.ActivationFunctionType
AX_X = mybir.AxisListType.X

N = 3125
E = 103125
D = 64
M = 8
P = 125
NB = N // P
NT = E // P
TG = 3
NG = NT // TG
GE = TG * P
PAIRS = NG // 2
TRASH = N
ROWS = N + P
IC = 75
NIC = NT // IC
DC = D + 1
ZC = M * D + M
CB = 4
NCH = -(-NB // CB)
CW = CB * P
EPS = 1e-5


def chunk_blocks(c):
    return range(c * CB, min(NB, c * CB + CB))


def chunk_cols(c):
    return c * CW, min(N, c * CW + CW)


def build_gnn(nc, a, out):
    tA = nc.dram_tensor("table_src", (N, D), F32, kind="Internal").ap()
    tB = nc.dram_tensor("table_dst", (N, D), F32, kind="Internal").ap()
    tU = nc.dram_tensor("table_logit_src", (N, M), F32, kind="Internal").ap()
    tZ = nc.dram_tensor("table_value_dst", (N, ZC), F32, kind="Internal").ap()
    sum0 = [nc.dram_tensor(f"sum0_{q}", (ROWS, DC), F32, kind="Internal").ap() for q in range(TG)]
    sum1 = [nc.dram_tensor(f"sum1_{q}", (ROWS, D), F32, kind="Internal").ap() for q in range(TG)]

    with ExitStack() as ctx:
        def sb(name, shape, dt=F32):
            return ctx.enter_context(nc.sbuf_tensor(name, shape, dt))

        def sem(name):
            return ctx.enter_context(nc.semaphore(name))

        bank = [ctx.enter_context(nc.psum_tensor(f"bank{k}", [128, 512], F32)) for k in range(8)]

        ident = sb("ident", [128, 128])
        tri = sb("tri", [P, P])
        trash = sb("trash", [P, 1])
        w_ab = sb("w_ab", [DC, 2 * D])
        w_ex = sb("w_ex", [128, D])
        w2 = sb("w2", [DC, D])
        w3 = sb("w3", [DC, D])
        wn1h = sb("wn1h", [DC, D])
        wn1a = sb("wn1a", [D, D])
        wn2 = sb("wn2", [DC, D])
        wn3 = sb("wn3", [DC, D])
        w_z = sb("w_z", [D, M, D])
        w_u = sb("w_u", [DC, 2 * M])
        vb = sb("vb", [P, D])
        eps_col = sb("eps_col", [P, 1])

        raw = sb("raw", [IC, 3, NIC, P])
        rawi = sb("rawi", [IC, 2, NIC, P], I32)
        src_i = sb("src_i", [P, NT + 2 * TG], I32)
        dst_i = sb("dst_i", [P, NT + 2 * TG], I32)
        src_f = sb("src_f", [P, NT])
        dst_f = sb("dst_f", [P, NT])
        wgt = sb("wgt", [P, NT])

        x = sb("x", [P, NB, D])
        xc = sb("xc", [P, NB, D])
        h = sb("h", [P, NB, D])
        sq = sb("sq", [P, NB, D])
        st = sb("st", [P, 6, NB])
        hT = sb("hT", [DC, N])
        sT = sb("sT", [DC, N])
        nT1 = sb("nT1", [DC, N])
        nT2 = sb("nT2", [DC, N])
        ab = sb("ab", [P, NB, 2 * D])
        sm = sb("sm", [P, TG, NB, DC])
        zero = sb("zero", [P, NB + 1, DC])
        zrow = sb("zrow", [P, 2, ZC])
        urow = sb("urow", [P, NB, M])

        X = sb("X", [P, 2, TG, 2 * D])
        Y = sb("Y", [P, 2, TG, D])
        XT = sb("XT", [128, 2, GE])
        H1 = sb("H1", [DC, 2, GE])
        H2 = sb("H2", [P, 2, TG, DC])
        KB = sb("KB", [P, 2, GE], I32)
        S = sb("S", [P, 2, TG, P])
        SL = sb("SL", [P, TG, P])
        dd = sb("dd", [P, 4, TG])
        C = sb("C", [P, 2, TG, DC])
        C1 = sb("C1", [P, 2, TG, D])
        slot_s = sb("slot_s", [P, 2, TG], I32)
        slot_d = sb("slot_d", [P, 2, TG], I32)
        slot_c = sb("slot_c", [P, 2, TG], I32)
        U = sb("U", [P, 2, TG, M])
        Z = sb("Z", [P, 2, TG, ZC])
        L = sb("L", [P, 2, TG, M])
        EX = sb("EX", [P, 2, TG, M])
        r4 = sb("r4", [P, 4, TG])

        weights_in = sem("weights_in")
        idx_in = sem("idx_in")
        x_in = sem("x_in")
        const_ready = sem("const_ready")
        pool_memset = sem("pool_memset")
        dve_step = sem("dve_step")
        act_step = sem("act_step")
        pe_step = sem("pe_step")
        zero_out = sem("zero_out")
        table_out = sem("table_out")
        z_out = [sem(f"z_out{k}") for k in range(2)]
        sums_in = sem("sums_in")
        y_out = sem("y_out")
        rows_in = [[sem(f"rows_in{l}_{j}") for j in range(2)] for l in range(2)]
        gat_a = [[[sem(f"gather{l}_a{j}{q}") for q in range(TG)] for j in range(2)] for l in range(2)]
        gat_b = [[[sem(f"gather{l}_b{j}{q}") for q in range(TG)] for j in range(2)] for l in range(2)]
        scat = [[sem(f"scatter{l}_{q}") for q in range(TG)] for l in range(2)]
        retired = [sem(f"retired{l}") for l in range(2)]
        pool_go = sem("pool_go")
        slots_ready = [sem(f"slots_ready{l}") for l in range(2)]
        dve_g = [sem(f"dve_group{l}") for l in range(2)]
        act_g = [sem(f"act_group{l}") for l in range(2)]
        pe_g = [sem(f"pe_group{l}") for l in range(2)]

        D0_S, D0_SL, D0_CNT, D0_ONE, D0_OFF, D0_MUL, D0_IDX, D0_SUM, D0_C, DVE0 = *range(1, 10), 9
        A0_XT, A0_H1, A0_H2, ACT0 = 1, 2, 3, 3
        P0_T, P0_H1, P0_H2, P0_C, PE0 = 1, 2, 3, 4, 4
        (D1_S, D1_SL, D1_CNT, D1_ONE, D1_OFF, D1_MUL, D1_IDX, D1_LOG, D1_MAX, D1_SUB, D1_SUM, D1_REC, D1_QS,
         D1_QW, D1_Z, D1_C, DVE1) = *range(1, 17), 16
        A1_EXP, ACT1 = 1, 1
        P1_C, PE1 = 1, 1

        class Steps:
            def __init__(self):
                self.n, self.at = 0, {}

            def add(self, *names):
                for name in names:
                    self.n += 1
                    self.at[name] = self.n

        dv, ac, pe_ = Steps(), Steps(), Steps()
        dv.add("rawf", "ones0", "ones1", "ones2", "onesH1", "onesH2", "neg_u", "pads", "padd", "w_ex")
        for k in range(6):
            dv.add(("turned", k), ("turned_f", k))
        dv.add("mean", "xc", "sq", "var", "rstd", "norm", "relu")
        for c in range(NCH):
            dv.add(("ab", c))
        dv.add("s01", "s012")
        for c in range(NCH):
            dv.add(("agg", c))
        for c in range(NCH):
            dv.add(("x1", c))
        dv.add("mean'", "xc'", "sq'", "var'", "rstd'", "norm'", "relu'")
        for b in range(NB):
            dv.add(("z", b), ("u", b))
        dv.add("y01", "y012", "yx", "y")
        ac.add("std")
        for c in range(NCH):
            ac.add(("hT", c))
        for c in range(NCH):
            ac.add(("sT", c))
        for c in range(NCH):
            ac.add(("g1", c))
        for c in range(NCH):
            ac.add(("g2", c))
        ac.add("std'")
        for c in range(NCH):
            ac.add(("h'T", c))
        for k in range(6):
            pe_.add(("turn", k))
        for c in range(NCH):
            pe_.add(("hT", c))
        for c in range(NCH):
            pe_.add(("ab", c))
        for c in range(NCH):
            pe_.add(("sT", c))
        for s in ("agg", "g1", "g2", "x1"):
            for c in range(NCH):
                pe_.add((s, c))
        for c in range(NCH):
            pe_.add(("h'T", c))
        for b in range(NB):
            pe_.add(("z", b))

        def done_dve(eng, name):
            eng.wait_ge(dve_step, dv.at[name])

        def done_act(eng, name):
            eng.wait_ge(act_step, ac.at[name])

        def done_pe(eng, name):
            eng.wait_ge(pe_step, pe_.at[name])

        edge_in = a["edge_attr_64"]
        nodes = "(b p) f -> p b f"
        WL = 19

        block = ctx.enter_context(nc.Block())

        @block.sync
        def _(sp):
            sp.dma_start(rawi[:, 0], a["src"].rearrange("(c q p) -> q c p", q=IC, p=P)).then_inc(idx_in, 16)
            sp.dma_start(rawi[:, 1], a["dst"].rearrange("(c q p) -> q c p", q=IC, p=P)).then_inc(idx_in, 16)
            sp.dma_start(raw[:, 2], a["edge_weight"].rearrange("(c q p) -> q c p", q=IC, p=P)).then_inc(idx_in, 16)
            sp.dma_start(x[:], a["x"].rearrange(nodes, p=P)).then_inc(x_in, 16)
            We1 = a["L0_gnn_We1"]
            loads = [
                (w_ex[0:D, :], We1[0:D, :]),
                (w_ab[0:D, 0:D], We1[D:2 * D, :]),
                (w_ab[0:D, D:2 * D], We1[2 * D:3 * D, :]),
                (w_ab[D:DC, 0:D], a["L0_gnn_be1"].unsqueeze(0)),
                (w2[0:D, :], a["L0_gnn_We2"]), (w2[D:DC, :], a["L0_gnn_be2"].unsqueeze(0)),
                (w3[0:D, :], a["L0_gnn_We3"]), (w3[D:DC, :], a["L0_gnn_be3"].unsqueeze(0)),
                (wn1h[0:D, :], a["L0_gnn_Wn1"][0:D, :]), (wn1h[D:DC, :], a["L0_gnn_bn1"].unsqueeze(0)),
                (wn1a[:], a["L0_gnn_Wn1"][D:2 * D, :]),
                (wn2[0:D, :], a["L0_gnn_Wn2"]), (wn2[D:DC, :], a["L0_gnn_bn2"].unsqueeze(0)),
                (wn3[0:D, :], a["L0_gnn_Wn3"]), (wn3[D:DC, :], a["L0_gnn_bn3"].unsqueeze(0)),
                (w_z[:], a["L1_gnn_var_w"].rearrange("m c d -> c m d")),
                (w_u[0:D, M:2 * M], a["L1_gnn_var_u"]), (w_u[D:DC, M:2 * M], a["L1_gnn_var_c"].unsqueeze(0)),
                (vb[:], a["L1_gnn_var_b"].partition_broadcast(P)),
            ]
            sp.wait_ge(pool_memset, 1)
            for dst, src in loads:
                sp.dma_start(dst, src).then_inc(weights_in, 16)

            for q in range(TG):
                sp.dma_start(sum0[q].rearrange(nodes, p=P), zero[:]).then_inc(zero_out, 16)
                sp.dma_start(sum1[q].rearrange(nodes, p=P), zero[:, :, 0:D]).then_inc(zero_out, 16)

            done_dve(sp, ("ab", NCH - 1))
            sp.dma_start(tA.rearrange(nodes, p=P), ab[:, :, 0:D]).then_inc(table_out, 16)
            sp.dma_start(tB.rearrange(nodes, p=P), ab[:, :, D:2 * D]).then_inc(table_out, 16)

            def rows0(i, j):
                g = 2 * i + j
                sp.wait_ge(pe_g[0], g * PE0 + P0_T)
                sp.wait_ge(dve_g[0], g * DVE0 + D0_S)
                sp.dma_start(X[:, j, :, 0:D], edge_in[bass.ds(g * GE, GE), :].rearrange("(q p) f -> p q f", p=P)
                             ).then_inc(rows_in[0][j], 16)
                sp.dma_start(KB[:, j, :], a["dst"][bass.ds(g * GE, GE)].partition_broadcast(P)
                             ).then_inc(rows_in[0][j], 16)

            with sp.Fori(0, PAIRS) as i:
                rows0(i, 0)
                rows0(i, 1)
            rows0(PAIRS, 0)

            for q in range(TG):
                sp.wait_ge(scat[0][q], 16 * NG)
            for q in range(TG):
                sp.dma_start(sm[:, q], sum0[q][0:N, :].rearrange(nodes, p=P)).then_inc(sums_in, 16)

            for b in range(NB):
                done_dve(sp, ("u", b))
                sp.dma_start(tZ[b * P:(b + 1) * P, :], zrow[:, b % 2, :]).then_inc(z_out[b % 2], 16)
            sp.dma_start(tU.rearrange(nodes, p=P), urow[:]).then_inc(table_out, 16)

            def rows1(i, j):
                g = 2 * i + j
                sp.wait_ge(dve_g[1], g * DVE1 + D1_S)
                sp.dma_start(KB[:, j, :], a["src"][bass.ds(g * GE, GE)].partition_broadcast(P)
                             ).then_inc(rows_in[1][j], 16)

            with sp.Fori(0, PAIRS) as i:
                rows1(i, 0)
                rows1(i, 1)
            rows1(PAIRS, 0)

            for q in range(TG):
                sp.wait_ge(scat[1][q], 16 * NG)
            for q in range(TG):
                sp.dma_start(sm[:, q, :, 0:D], sum1[q][0:N, :].rearrange(nodes, p=P)).then_inc(sums_in, 16)
            done_dve(sp, "y")
            sp.dma_start(out.rearrange(nodes, p=P), h[:]).then_inc(y_out, 16)
            sp.wait_ge(y_out, 16)

        @block.gpsimd
        def _(pool):
            pool.memset(w_ab[:], 0.0)
            pool.memset(w_u[:], 0.0)
            pool.memset(zero[:], 0.0).then_inc(pool_memset, 1)
            pool.memset(ident[:], 0.0).then_inc(const_ready, 1)
            pool.wait_ge(const_ready, 1)
            pool.affine_select(out=ident[:], in_=ident[:], compare_op=ALU.not_equal, fill=1.0, base=0,
                               pattern=[[-1, 128]], channel_multiplier=1).then_inc(const_ready, 1)
            pool.wait_ge(const_ready, 2)
            pool.memset(tri[:], 1.0).then_inc(const_ready, 1)
            pool.wait_ge(const_ready, 3)
            pool.affine_select(out=tri[:], in_=tri[:], compare_op=ALU.is_gt, fill=0.0, base=0,
                               pattern=[[-1, P]], channel_multiplier=1).then_inc(const_ready, 1)
            pool.iota(trash[:], [[0, 1]], base=TRASH, channel_multiplier=1,
                      allow_small_or_imprecise_dtypes=True).then_inc(const_ready, 1)

            def gathers(l, i, j):
                g = 2 * i + j
                pool.wait_ge(slots_ready[l], g + 1)
                pool.sem_inc(pool_go, 1)
                for q in range(TG):
                    to_a = X[:, j, q, D:2 * D] if l == 0 else U[:, j, q, :]
                    to_b = Y[:, j, q, :] if l == 0 else Z[:, j, q, :]
                    pool.indirect_dma_start(to_a, None, tA if l == 0 else tU,
                                            bass.IndirectOffsetOnAxis(ap=slot_s[:, j, q:q + 1], axis=0)
                                            ).then_inc(gat_a[l][j][q], 16)
                    pool.indirect_dma_start(to_b, None, tB if l == 0 else tZ,
                                            bass.IndirectOffsetOnAxis(ap=slot_d[:, j, q:q + 1], axis=0)
                                            ).then_inc(gat_b[l][j][q], 16)

            def scatters(l, i, j):
                g = 2 * i + j
                for q in range(TG):
                    pool.wait_ge(scat[l][q], 16 * g)
                    pool.sem_inc(retired[l], 1)
                pool.wait_ge(dve_g[l], g * (DVE0, DVE1)[l] + (D0_C, D1_C)[l] + 2 * (DVE0, DVE1)[l])
                pool.sem_inc(pool_go, 1)
                for q in range(TG):
                    pool.indirect_dma_start((sum0, sum1)[l][q],
                                            bass.IndirectOffsetOnAxis(ap=slot_c[:, j, q:q + 1], axis=0),
                                            (C, C1)[l][:, j, q, :], None, compute_op=ALU.add
                                            ).then_inc(scat[l][q], 16)

            for l in range(2):
                if l == 0:
                    pool.wait_ge(table_out, 32)
                    pool.wait_ge(zero_out, 16 * 2 * TG)
                else:
                    pool.wait_ge(table_out, 48)
                    pool.wait_ge(z_out[0], 16 * (NB - NB // 2))
                    pool.wait_ge(z_out[1], 16 * (NB // 2))
                gathers(l, 0, 0)
                with pool.Fori(0, PAIRS) as i:
                    gathers(l, i, 1)
                    scatters(l, i, 0)
                    gathers(l, i + 1, 0)
                    scatters(l, i, 1)
                scatters(l, PAIRS, 0)

        @block.scalar
        def _(act):
            def norm_std(name, var):
                done_dve(act, var)
                act.activation(st[:, 2], st[:, 1], ACT.Sqrt, bias=eps_col[:, 0:1], scale=1.0 / D).then_inc(act_step, 1)

            def slots(l, i, j):
                g = 2 * i + j
                act.copy(slot_s[:, j, :], src_i[:, bass.ds(g * TG, TG)])
                act.copy(slot_d[:, j, :], dst_i[:, bass.ds(g * TG, TG)]).then_inc(slots_ready[l], 1)

            norm_std("std", "var")
            for c in range(NCH):
                lo, hi = chunk_cols(c)
                done_pe(act, ("hT", c))
                act.copy(hT[0:D, lo:hi], bank[c % 2][0:D, 0:hi - lo]).then_inc(act_step, 1)

            def group0(i, j):
                g = 2 * i + j
                act.wait_ge(pe_g[0], (g + 2) * PE0 + P0_T)
                act.copy(XT[:, j, :], bank[j][:, 0:GE]).then_inc(act_g[0], 1)
                slots(0, i + 1, j)
                act.wait_ge(pe_g[0], (g + 2) * PE0 + P0_H1)
                act.activation(H1[0:D, j, :], bank[2 + j][0:D, 0:GE], ACT.Relu).then_inc(act_g[0], 1)
                act.wait_ge(pe_g[0], (g + 2) * PE0 + P0_H2)
                act.activation(H2[:, j, :, 0:D], bank[4 + j][0:P, 0:TG * D].rearrange("p (q f) -> p q f", q=TG),
                               ACT.Relu).then_inc(act_g[0], 1)

            act.sem_inc(act_g[0], 2 * ACT0)
            act.sem_inc(act_g[1], 2 * ACT1)
            done_dve(act, "padd")
            done_dve(act, ("turned_f", 5))
            slots(0, 0, 0)
            slots(0, 0, 1)
            with act.Fori(0, PAIRS) as i:
                group0(i, 0)
                group0(i, 1)
            group0(PAIRS, 0)

            for c in range(NCH):
                lo, hi = chunk_cols(c)
                done_pe(act, ("sT", c))
                act.copy(sT[:, lo:hi], bank[c % 2][0:DC, 0:hi - lo]).then_inc(act_step, 1)
            for s, to in (("g1", nT1), ("g2", nT2)):
                for c in range(NCH):
                    lo, hi = chunk_cols(c)
                    done_pe(act, (s, c))
                    act.activation(to[0:D, lo:hi], bank[c % 2][0:D, 0:hi - lo], ACT.Relu).then_inc(act_step, 1)
            norm_std("std'", "var'")
            for c in range(NCH):
                lo, hi = chunk_cols(c)
                done_pe(act, ("h'T", c))
                act.copy(hT[0:D, lo:hi], bank[c % 2][0:D, 0:hi - lo]).then_inc(act_step, 1)

            def group1(i, j):
                g = 2 * i + j
                act.wait_ge(dve_g[1], (g + 2) * DVE1 + D1_SUB)
                act.activation(EX[:, j], L[:, j], ACT.Exp).then_inc(act_g[1], 1)
                act.wait_ge(pe_g[1], (g + 2) * PE1 + P1_C)
                slots(1, i + 1, j)

            slots(1, 0, 0)
            slots(1, 0, 1)
            with act.Fori(0, PAIRS) as i:
                group1(i, 0)
                group1(i, 1)
            group1(PAIRS, 0)

        @block.vector
        def _(dve):
            def step(ins):
                ins.then_inc(dve_step, 1)

            def layer_norm(t):
                step(dve.tensor_reduce(st[:, 0], x[:], AX_X, ALU.add))
                done_dve(dve, "mean" + t)
                step(dve.scalar_tensor_tensor(out=xc[:], in0=st[:, 0].unsqueeze(2).to_broadcast([P, NB, D]),
                                              scalar=-1.0 / D, in1=x[:], op0=ALU.mult, op1=ALU.add))
                done_dve(dve, "xc" + t)
                step(dve.tensor_tensor(sq[:], xc[:], xc[:], ALU.mult))
                done_dve(dve, "sq" + t)
                step(dve.tensor_reduce(st[:, 1], sq[:], AX_X, ALU.add))
                done_act(dve, "std" + t)
                step(dve.reciprocal(st[:, 3], st[:, 2]))
                done_dve(dve, "rstd" + t)
                step(dve.tensor_tensor(h[:], xc[:], st[:, 3].unsqueeze(2).to_broadcast([P, NB, D]), ALU.mult))
                done_dve(dve, "norm" + t)
                step(dve.tensor_scalar(h[:], h[:], 0.0, None, ALU.max))

            dve.memset(eps_col[:], EPS)
            dve.wait_ge(idx_in, 48)
            step(dve.tensor_copy(raw[:, 0:2], rawi[:]))
            step(dve.memset(hT[D:DC, :], 1.0))
            step(dve.memset(nT1[D:DC, :], 1.0))
            step(dve.memset(nT2[D:DC, :], 1.0))
            step(dve.memset(H1[D:DC, :, :], 1.0))
            step(dve.memset(H2[:, :, :, D:DC], 1.0))
            dve.wait_ge(weights_in, 16 * WL)
            step(dve.tensor_scalar(w_u[0:D, 0:M], w_u[0:D, M:2 * M], -1.0, None, ALU.mult))
            step(dve.memset(src_i[:, NT:], 0))
            step(dve.memset(dst_i[:, NT:], 0))
            dve.wait_ge(const_ready, 2)
            step(dve.tensor_copy(w_ex[D:2 * D, :], ident[D:2 * D, D:2 * D]))
            for k in range(6):
                what, half = k // 2, k % 2
                lo, hi = (0, 6 * IC) if half == 0 else (6 * IC, NT)
                done_pe(dve, ("turn", k))
                t = (src_i, dst_i, wgt)[what]
                tf = (src_f, dst_f, wgt)[what]
                step(dve.tensor_copy(t[:, lo:hi], bank[2 + k][0:P, 0:hi - lo]))
                if what == 2:
                    done_dve(dve, ("turned", k))
                step(dve.tensor_copy(tf[:, lo:hi], bank[2 + k][0:P, 0:hi - lo]))
            dve.wait_ge(x_in, 16)
            layer_norm("")
            for c in range(NCH):
                b = chunk_blocks(c)
                done_pe(dve, ("ab", c))
                step(dve.tensor_copy(ab[:, b[0]:b[-1] + 1, :],
                                     bank[c % 2][0:P, 0:len(b) * 2 * D].rearrange("p (b f) -> p b f", f=2 * D)))

            dve.sem_inc(dve_g[0], 2 * DVE0)
            dve.sem_inc(dve_g[1], 2 * DVE1)
            dve.wait_ge(const_ready, 5)

            def equal_rows(l, i, j, keys):
                g = 2 * i + j
                base, s = (g + 2) * (DVE0, DVE1)[l], dve_g[l]
                kf = keys[:, bass.ds(g * TG, TG)]
                dve.wait_ge(rows_in[l][j], (i + 1) * (32, 16)[l])
                dve.wait_ge(pe_g[l], (g + 1) * (PE0, PE1)[l])
                dve.tensor_tensor(S[:, j], KB[:, j, :].rearrange("p (q f) -> p q f", q=TG),
                                  kf.unsqueeze(2).to_broadcast([P, TG, P]), ALU.is_equal).then_inc(s, 1)
                dve.wait_ge(s, base + D0_S)
                dve.tensor_tensor(SL[:], S[:, j], tri[:].unsqueeze(1).to_broadcast([P, TG, P]),
                                  ALU.mult).then_inc(s, 1)
                dve.wait_ge(s, base + D0_SL)
                dve.tensor_reduce(dd[:, 0], SL[:], AX_X, ALU.add).then_inc(s, 1)
                dve.wait_ge(s, base + D0_CNT)
                dve.tensor_scalar(dd[:, 1], dd[:, 0], 1.0, None, ALU.min).then_inc(s, 1)
                dve.tensor_scalar(dd[:, 2], kf, -1.0, trash[:, 0:1], ALU.mult, ALU.add).then_inc(s, 1)
                dve.wait_ge(s, base + D0_OFF)
                dve.tensor_tensor(dd[:, 3], dd[:, 1], dd[:, 2], ALU.mult).then_inc(s, 1)
                dve.wait_ge(s, base + D0_MUL)
                dve.wait_ge(retired[l], TG * g)
                dve.tensor_tensor(slot_c[:, j, :], dd[:, 3], kf, ALU.add).then_inc(s, 1)

            def group0(i, j):
                g = 2 * i + j
                base = (g + 2) * DVE0
                equal_rows(0, i, j, dst_f)
                for q in range(TG):
                    dve.wait_ge(gat_a[0][j][q], (i + 1) * 16)
                    dve.wait_ge(gat_b[0][j][q], (i + 1) * 16)
                dve.tensor_tensor(X[:, j, :, D:2 * D], X[:, j, :, D:2 * D], Y[:, j], ALU.add).then_inc(dve_g[0], 1)
                dve.wait_ge(pe_g[0], (g + 2) * PE0 + P0_C)
                dve.tensor_copy(C[:, j], bank[6 + j][0:P, 0:TG * DC].rearrange("p (q f) -> p q f", q=TG)
                                ).then_inc(dve_g[0], 1)

            with dve.Fori(0, PAIRS) as i:
                group0(i, 0)
                group0(i, 1)
            group0(PAIRS, 0)

            dve.wait_ge(sums_in, 16 * TG)
            step(dve.tensor_tensor(sm[:, 0], sm[:, 0], sm[:, 1], ALU.add))
            done_dve(dve, "s01")
            step(dve.tensor_tensor(sm[:, 0], sm[:, 0], sm[:, 2], ALU.add))
            for c in range(NCH):
                lo, hi = chunk_cols(c)
                done_pe(dve, ("agg", c))
                step(dve.tensor_copy(nT2[0:D, lo:hi], bank[2 + c % 2][0:D, 0:hi - lo]))
            for c in range(NCH):
                b = chunk_blocks(c)
                done_pe(dve, ("x1", c))
                step(dve.tensor_tensor(x[:, b[0]:b[-1] + 1, :], x[:, b[0]:b[-1] + 1, :],
                                       bank[4 + c % 2][0:P, 0:len(b) * D].rearrange("p (b f) -> p b f", f=D), ALU.add))
            done_dve(dve, ("x1", NCH - 1))
            layer_norm("'")
            for b in range(NB):
                done_pe(dve, ("z", b))
                if b >= 2:
                    dve.wait_ge(z_out[b % 2], 16 * (b // 2))
                step(dve.tensor_copy(zrow[:, b % 2, 0:M * D], bank[2 * (b % 2)][0:P, :]))
                dve.tensor_copy(urow[:, b, :], bank[2 * (b % 2) + 1][0:P, M:2 * M])
                step(dve.tensor_copy(zrow[:, b % 2, M * D:], bank[2 * (b % 2) + 1][0:P, 0:M]))

            def group1(i, j):
                g = 2 * i + j
                base, s = (g + 2) * DVE1, dve_g[1]
                equal_rows(1, i, j, src_f)
                for q in range(TG):
                    dve.wait_ge(gat_a[1][j][q], (i + 1) * 16)
                    dve.wait_ge(gat_b[1][j][q], (i + 1) * 16)
                dve.tensor_tensor(L[:, j], U[:, j], Z[:, j, :, M * D:], ALU.add).then_inc(s, 1)
                dve.wait_ge(s, base + D1_LOG)
                dve.tensor_reduce(r4[:, 0], L[:, j], AX_X, ALU.max).then_inc(s, 1)
                dve.wait_ge(s, base + D1_MAX)
                dve.tensor_tensor(L[:, j], L[:, j], r4[:, 0].unsqueeze(2).to_broadcast([P, TG, M]),
                                  ALU.subtract).then_inc(s, 1)
                dve.wait_ge(act_g[1], (g + 2) * ACT1 + A1_EXP)
                dve.tensor_reduce(r4[:, 1], EX[:, j], AX_X, ALU.add).then_inc(s, 1)
                dve.wait_ge(s, base + D1_SUM)
                dve.reciprocal(r4[:, 2], r4[:, 1]).then_inc(s, 1)
                dve.wait_ge(s, base + D1_REC)
                dve.tensor_tensor(r4[:, 3], r4[:, 2], wgt[:, bass.ds(g * TG, TG)], ALU.mult).then_inc(s, 1)
                dve.wait_ge(s, base + D1_QS)
                dve.tensor_tensor(EX[:, j], EX[:, j], r4[:, 3].unsqueeze(2).to_broadcast([P, TG, M]),
                                  ALU.mult).then_inc(s, 1)
                dve.wait_ge(s, base + D1_QW)
                for q in range(TG):
                    zq = Z[:, j, q, 0:M * D].rearrange("p (m f) -> p m f", m=M)
                    last = dve.tensor_tensor(zq, zq, EX[:, j, q].unsqueeze(2).to_broadcast([P, M, D]), ALU.mult)
                last.then_inc(s, 1)
                dve.wait_ge(pe_g[1], (g + 2) * PE1 + P1_C)
                dve.tensor_copy(C1[:, j], bank[6 + j][0:P, 0:TG * D].rearrange("p (q f) -> p q f", q=TG)
                                ).then_inc(s, 1)

            with dve.Fori(0, PAIRS) as i:
                group1(i, 0)
                group1(i, 1)
            group1(PAIRS, 0)

            dve.wait_ge(sums_in, 32 * TG)
            step(dve.tensor_tensor(h[:], sm[:, 0, :, 0:D], sm[:, 1, :, 0:D], ALU.add))
            done_dve(dve, "y01")
            step(dve.tensor_tensor(h[:], h[:], sm[:, 2, :, 0:D], ALU.add))
            done_dve(dve, "y012")
            step(dve.tensor_tensor(h[:], h[:], vb[:].unsqueeze(1).to_broadcast([P, NB, D]), ALU.add))
            done_dve(dve, "yx")
            step(dve.tensor_tensor(h[:], h[:], x[:], ALU.add))

        @block.tensor
        def _(pe):
            def turn_nodes(name, from_, width, act_name):
                for c in range(NCH):
                    if c >= 2:
                        done_act(pe, (act_name, c - 2))
                    for n, b in enumerate(chunk_blocks(c)):
                        last = pe.transpose(bank[c % 2][0:width, n * P:(n + 1) * P], from_(b), ident[0:P, 0:P])
                    last.then_inc(pe_step, 1)

            pe.wait_ge(const_ready, 2)
            done_dve(pe, "rawf")
            for k in range(6):
                what, half = k // 2, k % 2
                for n, c in enumerate(range(0, 6) if half == 0 else range(6, NIC)):
                    last = pe.transpose(bank[2 + k][0:P, n * IC:(n + 1) * IC], raw[:, what, c, :], ident[0:IC, 0:IC])
                last.then_inc(pe_step, 1)

            done_dve(pe, "relu")
            turn_nodes("hT", lambda b: h[:, b, :], D, "hT")
            done_act(pe, ("hT", NCH - 1))
            for c in range(NCH):
                if c >= 2:
                    done_dve(pe, ("ab", c - 2))
                for n, b in enumerate(chunk_blocks(c)):
                    last = pe.matmul(bank[c % 2][0:P, n * 2 * D:(n + 1) * 2 * D], hT[:, b * P:(b + 1) * P], w_ab[:],
                                     start=True, stop=True)
                last.then_inc(pe_step, 1)
            done_dve(pe, ("ab", NCH - 1))

            pe.sem_inc(pe_g[0], 2 * PE0)
            pe.sem_inc(pe_g[1], 2 * PE1)

            def group0(i, j):
                g = 2 * i + j
                pe.wait_ge(rows_in[0][j], (i + 1) * 32)
                pe.wait_ge(dve_g[0], (g + 2) * DVE0 + D0_SUM)
                for q in range(TG):
                    last = pe.transpose(bank[j][:, q * P:(q + 1) * P], X[:, j, q, :], ident[0:P, 0:P])
                last.then_inc(pe_g[0], 1)
                pe.wait_ge(act_g[0], (g + 2) * ACT0 + A0_XT)
                pe.matmul(bank[2 + j][0:D, 0:GE], w_ex[:], XT[:, j, :], start=True, stop=True).then_inc(pe_g[0], 1)
                pe.wait_ge(act_g[0], (g + 2) * ACT0 + A0_H1)
                for q in range(TG):
                    last = pe.matmul(bank[4 + j][0:P, q * D:(q + 1) * D], H1[:, j, q * P:(q + 1) * P], w2[:],
                                     start=True, stop=True)
                last.then_inc(pe_g[0], 1)
                pe.wait_ge(act_g[0], (g + 2) * ACT0 + A0_H2)
                for q in range(TG):
                    last = pe.matmul(bank[6 + j][0:P, q * DC:(q + 1) * DC], S[:, j, q, :], H2[:, j, q, :],
                                     start=True, stop=True)
                last.then_inc(pe_g[0], 1)

            with pe.Fori(0, PAIRS) as i:
                group0(i, 0)
                group0(i, 1)
            group0(PAIRS, 0)

            done_dve(pe, "s012")
            turn_nodes("sT", lambda b: sm[:, 0, b, :], DC, "sT")
            done_act(pe, ("sT", NCH - 1))
            for c in range(NCH):
                lo, hi = chunk_cols(c)
                if c >= 2:
                    done_dve(pe, ("agg", c - 2))
                pe.matmul(bank[2 + c % 2][0:D, 0:hi - lo], w3[:], sT[:, lo:hi], start=True, stop=True
                          ).then_inc(pe_step, 1)
            done_dve(pe, ("agg", NCH - 1))
            for c in range(NCH):
                lo, hi = chunk_cols(c)
                if c >= 2:
                    done_act(pe, ("g1", c - 2))
                pe.matmul(bank[c % 2][0:D, 0:hi - lo], wn1h[:], hT[:, lo:hi], start=True, stop=False)
                pe.matmul(bank[c % 2][0:D, 0:hi - lo], wn1a[:], nT2[0:D, lo:hi], start=False, stop=True
                          ).then_inc(pe_step, 1)
            done_act(pe, ("g1", NCH - 1))
            for c in range(NCH):
                lo, hi = chunk_cols(c)
                if c >= 2:
                    done_act(pe, ("g2", c - 2))
                pe.matmul(bank[c % 2][0:D, 0:hi - lo], wn2[:], nT1[:, lo:hi], start=True, stop=True
                          ).then_inc(pe_step, 1)
            done_act(pe, ("g2", NCH - 1))
            for c in range(NCH):
                if c >= 2:
                    done_dve(pe, ("x1", c - 2))
                for n, b in enumerate(chunk_blocks(c)):
                    last = pe.matmul(bank[4 + c % 2][0:P, n * D:(n + 1) * D], nT2[:, b * P:(b + 1) * P], wn3[:],
                                     start=True, stop=True)
                last.then_inc(pe_step, 1)
            done_dve(pe, "relu'")
            turn_nodes("h'T", lambda b: h[:, b, :], D, "h'T")
            done_act(pe, ("h'T", NCH - 1))
            for b in range(NB):
                if b >= 2:
                    done_dve(pe, ("u", b - 2))
                pe.matmul(bank[2 * (b % 2)][0:P, :], hT[0:D, b * P:(b + 1) * P],
                          w_z[:].rearrange("c m d -> c (m d)"), start=True, stop=True)
                pe.matmul(bank[2 * (b % 2) + 1][0:P, 0:2 * M], hT[:, b * P:(b + 1) * P], w_u[:],
                          start=True, stop=True).then_inc(pe_step, 1)
            done_dve(pe, ("u", NB - 1))

            def group1(i, j):
                g = 2 * i + j
                pe.wait_ge(dve_g[1], (g + 2) * DVE1 + D1_Z)
                for q in range(TG):
                    for m in range(M):
                        last = pe.matmul(bank[6 + j][0:P, q * D:(q + 1) * D], S[:, j, q, :],
                                         Z[:, j, q, m * D:(m + 1) * D], start=(m == 0), stop=(m == M - 1))
                last.then_inc(pe_g[1], 1)

            with pe.Fori(0, PAIRS) as i:
                group1(i, 0)
                group1(i, 1)
            group1(PAIRS, 0)


NAMES = ["x", "src", "dst", "edge_attr_64", "edge_weight", "L0_gnn_We1", "L0_gnn_be1", "L0_gnn_We2", "L0_gnn_be2",
         "L0_gnn_We3", "L0_gnn_be3", "L0_gnn_Wn1", "L0_gnn_bn1", "L0_gnn_Wn2", "L0_gnn_bn2", "L0_gnn_Wn3",
         "L0_gnn_bn3", "L1_gnn_var_u", "L1_gnn_var_c", "L1_gnn_var_w", "L1_gnn_var_b"]


def kernel(**inputs):
    import numpy as _np
    import concourse.bacc as _bacc
    from concourse import mybir as _mybir
    from concourse.bass_utils import run_bass_kernel_spmd as _run

    nc = _bacc.Bacc("TRN2", target_bir_lowering=False, num_devices=1)
    arrays, aps = {}, {}
    for name in NAMES:
        v = _np.ascontiguousarray(inputs[name])
        arrays[f"in_{name}"] = v
        aps[name] = nc.dram_tensor(f"in_{name}", v.shape, _mybir.dt.from_np(v.dtype), kind="ExternalInput").ap()
    out = nc.dram_tensor("out_0", (N, D), _mybir.dt.float32, kind="ExternalOutput").ap()
    build_gnn(nc, aps, out)
    r = _run(nc, [arrays], core_ids=[0])
    return r.results[0]["out_0"]
```

```python
from contextlib import ExitStack

import concourse.bass as bass
from concourse import mybir

F32 = mybir.dt.float32
I32 = mybir.dt.int32
ALU = mybir.AluOpType
ACT = mybir.ActivationFunctionType
AX_X = mybir.AxisListType.X

N = 3125
E = 103125
D = 64
M = 8
P = 125
NB = N // P
NT = E // P
TG = 3
NG = NT // TG
GE = TG * P
PAIRS = NG // 2
TRASH = N
ROWS = N + P
IC = 75
NIC = NT // IC
DC = D + 1
ZC = M * D
RB = 4
TURNS = NG // RB
WG = 64
WT = 16
CB = 4
NCH = -(-NB // CB)
CW = CB * P
EPS = 1e-5


def chunk_blocks(c):
    return range(c * CB, min(NB, c * CB + CB))


def chunk_cols(c):
    return c * CW, min(N, c * CW + CW)


def build_gnn(nc, a, out):
    tA = nc.dram_tensor("table_src", (N, D), F32, kind="Internal").ap()
    tB = nc.dram_tensor("table_dst", (N, D), F32, kind="Internal").ap()
    tU = nc.dram_tensor("table_logit_src", (N, M), F32, kind="Internal").ap()
    tV = nc.dram_tensor("table_logit_dst", (N, M), F32, kind="Internal").ap()
    tZ = nc.dram_tensor("table_value_dst", (N * M, D), F32, kind="Internal").ap()
    tZrow = tZ.rearrange("(n m) f -> n (m f)", m=M)
    sum0 = [nc.dram_tensor(f"sum0_{q}", (ROWS, DC), F32, kind="Internal").ap() for q in range(TG)]
    sum1 = [nc.dram_tensor(f"sum1_{q}", (ROWS, D), F32, kind="Internal").ap() for q in range(TG)]

    with ExitStack() as ctx:
        def sb(name, shape, dt=F32):
            return ctx.enter_context(nc.sbuf_tensor(name, shape, dt))

        def sem(name):
            return ctx.enter_context(nc.semaphore(name))

        bank = [ctx.enter_context(nc.psum_tensor(f"bank{k}", [128, 512], F32)) for k in range(8)]

        ident = sb("ident", [128, 128])
        tri = sb("tri", [P, P])
        trash = sb("trash", [P, 1])
        w_ab = sb("w_ab", [DC, 2 * D])
        w_ex = sb("w_ex", [128, D])
        w2 = sb("w2", [DC, D])
        w3 = sb("w3", [DC, D])
        wn1h = sb("wn1h", [DC, D])
        wn1a = sb("wn1a", [D, D])
        wn2 = sb("wn2", [DC, D])
        wn3 = sb("wn3", [DC, D])
        w_z = sb("w_z", [D, M, D])
        w_u = sb("w_u", [DC, 2 * M])
        vb = sb("vb", [P, D])
        eps_col = sb("eps_col", [P, 1])
        ones = sb("ones", [1, P])
        iota_g = sb("iota_g", [P, WG])
        part = sb("part", [P, 1])

        src_i = sb("src_i", [P, NT + RB * TG], I32)
        dst_i = sb("dst_i", [P, NT + RB * TG], I32)
        src_f = sb("src_f", [P, NT])
        dst_f = sb("dst_f", [P, NT])
        wgt = sb("wgt", [P, NT])

        base_g = sb("base_g", [P, NG])
        base = sb("base", [P, NT])
        base_p = sb("base_p", [P, NG])
        rel_g = sb("rel_g", [P, NT])
        rel_t = sb("rel_t", [P, NT])
        base_gi = sb("base_gi", [1, NG], I32)
        base_ti = sb("base_ti", [1, NT], I32)
        span = sb("span", [P, 8])
        flag = sb("flag", [1, 4])
        flag_i = sb("flag_i", [1, 1], I32)
        slot_all = sb("slot_all", [P, NT], I32)

        x = sb("x", [P, NB, D])
        h = sb("h", [P, NB, D])
        st = sb("st", [P, 6, NB])
        hT = sb("hT", [DC, N])
        sT = sb("sT", [DC, N])
        nT2 = sb("nT2", [DC, N])
        ab = sb("ab", [P, NB, 2 * D])
        sm = sb("sm", [P, TG, NB, DC])
        sq = ab[:, :, 0:D]
        raw = sm[0:IC].rearrange("p q b f -> p (q b f)")[:, 0:3 * NT // IC * P].rearrange(
            "p (k c e) -> p k c e", k=3, e=P)
        rawi = ab[0:IC].rearrange("p b f -> p (b f)")[:, 0:2 * NT // IC * P].bitcast(I32).rearrange(
            "p (k c e) -> p k c e", k=2, e=P)
        zrow = sb("zrow", [P, 2, ZC])
        vrow = sb("vrow", [P, NB, M])
        urow = sb("urow", [P, NB, M])

        X = sb("X", [128, RB, TG, 2 * D])
        Y = sb("Y", [P, 2, TG, D])
        XT = sb("XT", [128, RB, GE])
        H1 = sb("H1", [DC, RB, GE])
        H2 = sb("H2", [P, RB, TG, DC])
        KB = sb("KB", [P, RB, GE], I32)
        S = sb("S", [P, RB, TG, P])
        SL = sb("SL", [P, TG, P])
        dd = sb("dd", [P, 4, TG])
        C = sb("C", [P, 2, TG, DC])
        C1 = sb("C1", [P, RB, TG, D])
        slot_s = sb("slot_s", [P, RB, TG], I32)
        slot_d = sb("slot_d", [P, 2, TG], I32)
        slot_c = sb("slot_c", [P, RB, TG], I32)
        U = sb("U", [P, RB, TG, M])
        V = sb("V", [P, 2, TG, M])
        Z = sb("Z", [P, 2, TG, ZC])
        zero = Z[:].rearrange("p j q f -> p (j q f)")[:, 0:(NB + 1) * DC].rearrange("p (b f) -> p b f", f=DC)
        KBT = sb("KBT", [WG, RB, GE], I32)
        OT = sb("OT", [WG, RB, GE])
        BW = sb("BW", [WG, RB, D])
        VW = sb("VW", [WG, RB, M])
        L = sb("L", [P, RB, TG, M])
        EX = sb("EX", [P, RB, TG, M])
        r4 = sb("r4", [P, 4, TG])
        flat = Z[:].rearrange("p j q f -> p (j q f)")
        at_oe, at_oh, at_end = RB * TG * WT * M, RB * TG * (WT * M + WG), RB * TG * (WT * M + WG + WT)
        Q = flat[:, 0:at_oe].rearrange("p (j q n m) -> p j q n m", j=RB, q=TG, m=M)
        OE = flat[:, at_oe:at_oh].rearrange("p (j q n) -> p j q n", j=RB, q=TG)
        OH = flat[:, at_oh:at_end].rearrange("p (j q n) -> p j q n", j=RB, q=TG)
        ZW = X[:, :, :, 0:D]
        R = XT

        weights_in = sem("weights_in")
        idx_in = sem("idx_in")
        x_in = sem("x_in")
        const_ready = sem("const_ready")
        pool_memset = sem("pool_memset")
        dve_step = sem("dve_step")
        act_step = sem("act_step")
        pe_step = sem("pe_step")
        zero_out = sem("zero_out")
        table_out = sem("table_out")
        z_out = [sem(f"z_out{k}") for k in range(2)]
        sums_in = sem("sums_in")
        y_out = sem("y_out")
        rows_in = [[sem(f"rows_in{l}_{j}") for j in range(2)] for l in range(2)]
        gat_a = [[[sem(f"gather{l}_a{j}{q}") for q in range(TG)] for j in range(RB)] for l in range(2)]
        gat_b = [[[sem(f"gather{l}_b{j}{q}") for q in range(TG)] for j in range(2)] for l in range(2)]
        scat = [[sem(f"scatter{l}_{q}") for q in range(TG)] for l in range(2)]
        retired = [sem(f"retired{l}") for l in range(2)]
        gat_v = [[sem(f"gather1_v{j}{q}") for q in range(TG)] for j in range(2)]
        pool_go = sem("pool_go")
        sp_go = sem("sp_go")
        sum_dve, sum_pe, sum_act = sem("sum_dve"), sem("sum_pe"), sem("sum_act")
        sums1_in = sem("sums1_in")
        sT_ready = sem("sT_ready")
        flag_ready = sem("flag_ready")
        win_dve = sem("win_dve")
        win_pe = sem("win_pe")
        x_load = [sem(f"x_load{j}") for j in range(RB)]
        kbt_load = [[sem(f"kbt_load{l}_{j}") for j in range(RB)] for l in range(2)]
        kb_load = [[sem(f"kb_load{l}_{j}") for j in range(RB)] for l in range(2)]
        bw_load = [sem(f"bw_load{j}") for j in range(RB)]
        zw_load = [sem(f"zw_load{j}") for j in range(RB)]
        f_T, f_XT, f_OT, f_h1, f_H1, f_h2, f_H2, f_OE, f_seg, f_acc, f_dd, f_chain = (
            sem(f"f_{n}") for n in ("T", "XT", "OT", "h1", "H1", "h2", "H2", "OE", "seg", "acc", "dd", "chain"))
        u_OT, u_V, u_S, u_L, u_EX, u_Q, u_R, u_RS, u_C, u_CS, u_chain, u_chain2 = (
            sem(f"u_{n}") for n in ("OT", "V", "S", "L", "EX", "Q", "R", "RS", "C", "CS", "chain", "chain2"))
        slots_ready = [sem(f"slots_ready{l}") for l in range(2)]
        dve_g = [sem(f"dve_group{l}") for l in range(2)]
        act_g = [sem(f"act_group{l}") for l in range(2)]
        pe_g = [sem(f"pe_group{l}") for l in range(2)]

        D0_S, D0_SL, D0_CNT, D0_ONE, D0_OFF, D0_MUL, D0_IDX, D0_SUM, D0_C, DVE0 = *range(1, 10), 9
        A0_XT, A0_H1, A0_H2, ACT0 = 1, 2, 3, 3
        P0_T, P0_H1, P0_H2, P0_C, PE0 = 1, 2, 3, 4, 4
        (D1_S, D1_SL, D1_CNT, D1_ONE, D1_OFF, D1_MUL, D1_IDX, D1_LOG, D1_MAX, D1_SUB, D1_SUM, D1_REC, D1_QS,
         D1_QW, D1_Z, D1_C, DVE1) = *range(1, 17), 16
        A1_EXP, ACT1 = 1, 1
        P1_C, PE1 = 1, 1

        class Steps:
            def __init__(self):
                self.n, self.at = 0, {}

            def add(self, *names):
                for name in names:
                    self.n += 1
                    self.at[name] = self.n

        dv, ac, pe_ = Steps(), Steps(), Steps()
        dv.add("rawf", "ones0", "ones2", "onesH1", "onesH2", "neg_u", "pads", "padd", "w_ex")
        for k in range(6):
            dv.add(("turned", k), ("turned_f", k))
        dv.add("mean", "xc", "sq", "var", "rstd", "norm", "relu")
        for c in range(NCH):
            dv.add(("ab", c))
        for c in range(NCH):
            dv.add(("agg", c))
        for c in range(NCH):
            dv.add(("x1", c))
        dv.add("mean'", "xc'", "sq'", "var'", "rstd'", "norm'", "relu'")
        for b in range(NB):
            dv.add(("z", b), ("u", b))
        dv.add("y01", "y012", "yx", "y")
        ac.add("std")
        for c in range(NCH):
            ac.add(("hT", c))
        for c in range(NCH):
            ac.add(("g1", c))
        for c in range(NCH):
            ac.add(("g2", c))
        ac.add("std'")
        for c in range(NCH):
            ac.add(("h'T", c))
        for k in range(6):
            pe_.add(("turn", k))
        for c in range(NCH):
            pe_.add(("hT", c))
        for c in range(NCH):
            pe_.add(("ab", c))
        for s in ("agg", "g1", "g2", "x1"):
            for c in range(NCH):
                pe_.add((s, c))
        for c in range(NCH):
            pe_.add(("h'T", c))
        for b in range(NB):
            pe_.add(("z", b))

        def done_dve(eng, name):
            eng.wait_ge(dve_step, dv.at[name])

        def done_act(eng, name):
            eng.wait_ge(act_step, ac.at[name])

        def done_pe(eng, name):
            eng.wait_ge(pe_step, pe_.at[name])

        DEPTH = 4

        def over_groups(eng, body):
            for s in range(2 * RB):
                body(s // RB, s % RB)
            with eng.Fori(2, TURNS) as t:
                for j in range(RB):
                    body(t, j)
            for s in range(TURNS * RB, NG + DEPTH):
                body(s // RB, s % RB)

        def back(step, t, j, k):
            jk = (j - k) % RB
            tk = t + (j - k - jk) // RB
            if not isinstance(t, int) or 0 <= RB * tk + jk < NG:
                step(tk, jk)

        def done(eng, counter, t, j, k=0):
            g = RB * t + j - k
            if not isinstance(t, int) or g >= 0:
                eng.wait_ge(counter, g + 1)

        def load_flag(eng):
            eng.wait_ge(flag_ready, 1)
            return eng.value_load(flag_i[0:1, 0:1], min_val=0, max_val=1)

        edge_in = a["edge_attr_64"]
        nodes = "(b p) f -> p b f"
        WIN_SPAN = 20
        WL = 19

        block = ctx.enter_context(nc.Block())

        @block.sync
        def _(sp):
            sp.dma_start(rawi[:, 0], a["src"].rearrange("(c q p) -> q c p", q=IC, p=P)).then_inc(idx_in, 16)
            sp.dma_start(rawi[:, 1], a["dst"].rearrange("(c q p) -> q c p", q=IC, p=P)).then_inc(idx_in, 16)
            sp.dma_start(raw[:, 2], a["edge_weight"].rearrange("(c q p) -> q c p", q=IC, p=P)).then_inc(idx_in, 16)
            sp.dma_start(x[:], a["x"].rearrange(nodes, p=P)).then_inc(x_in, 16)
            We1 = a["L0_gnn_We1"]
            loads = [
                (w_ex[0:D, :], We1[0:D, :]),
                (w_ab[0:D, 0:D], We1[D:2 * D, :]),
                (w_ab[0:D, D:2 * D], We1[2 * D:3 * D, :]),
                (w_ab[D:DC, 0:D], a["L0_gnn_be1"].unsqueeze(0)),
                (w2[0:D, :], a["L0_gnn_We2"]), (w2[D:DC, :], a["L0_gnn_be2"].unsqueeze(0)),
                (w3[0:D, :], a["L0_gnn_We3"]), (w3[D:DC, :], a["L0_gnn_be3"].unsqueeze(0)),
                (wn1h[0:D, :], a["L0_gnn_Wn1"][0:D, :]), (wn1h[D:DC, :], a["L0_gnn_bn1"].unsqueeze(0)),
                (wn1a[:], a["L0_gnn_Wn1"][D:2 * D, :]),
                (wn2[0:D, :], a["L0_gnn_Wn2"]), (wn2[D:DC, :], a["L0_gnn_bn2"].unsqueeze(0)),
                (wn3[0:D, :], a["L0_gnn_Wn3"]), (wn3[D:DC, :], a["L0_gnn_bn3"].unsqueeze(0)),
                (w_z[:], a["L1_gnn_var_w"].rearrange("m c d -> c m d")),
                (w_u[0:D, M:2 * M], a["L1_gnn_var_u"]), (w_u[D:DC, M:2 * M], a["L1_gnn_var_c"].unsqueeze(0)),
                (vb[:], a["L1_gnn_var_b"].partition_broadcast(P)),
            ]
            sp.wait_ge(pool_memset, 1)
            for dst, src in loads:
                sp.dma_start(dst, src).then_inc(weights_in, 16)

            for q in range(TG):
                sp.dma_start(sum0[q].rearrange(nodes, p=P), zero).then_inc(zero_out, 16)
                sp.dma_start(sum1[q].rearrange(nodes, p=P), zero[:, :, 0:D]).then_inc(zero_out, 16)

            done_dve(sp, ("ab", NCH - 1))
            sp.dma_start(tA.rearrange(nodes, p=P), ab[:, :, 0:D]).then_inc(table_out, 16)
            sp.dma_start(tB.rearrange(nodes, p=P), ab[:, :, D:2 * D]).then_inc(table_out, 16)

            flag_ = load_flag(sp)
            with sp.If(flag_):
                def rows0w(t, j):
                    g = RB * t + j
                    done(sp, f_T, t, j, RB)
                    sp.dma_start(X[0:P, j, :, 0:D], edge_in[bass.ds(g * GE, GE), :].rearrange("(q p) f -> p q f", p=P)
                                 ).then_inc(x_load[j], 16)
                    done(sp, f_OT, t, j, RB)
                    sp.sem_inc(sp_go, 1)
                    sp.dma_start(KBT[:, j, :], a["dst"][bass.ds(g * GE, GE)].partition_broadcast(WG)
                                 ).then_inc(kbt_load[0][j], 16)
                    done(sp, f_h1, t, j, RB)
                    sp.sem_inc(sp_go, 1)
                    first = sp.value_load(base_gi[0:1, bass.ds(g, 1)], min_val=0, max_val=N - WG)
                    sp.dma_start(BW[:, j, :], tB[bass.ds(first, WG), :]).then_inc(bw_load[j], 16)
                    done(sp, f_dd, t, j, RB)
                    sp.dma_start(KB[:, j, :], a["src"][bass.ds(g * GE, GE)].partition_broadcast(P)
                                 ).then_inc(kb_load[0][j], 16)

                sp.wait_ge(table_out, 32)
                over_groups(sp, lambda t, j: back(rows0w, t, j, 0))
            with sp.Else():
                def rows0(i, j):
                    g = 2 * i + j
                    sp.wait_ge(pe_g[0], g * PE0 + P0_T)
                    sp.wait_ge(dve_g[0], g * DVE0 + D0_S)
                    sp.dma_start(X[0:P, j, :, 0:D], edge_in[bass.ds(g * GE, GE), :].rearrange("(q p) f -> p q f", p=P)
                                 ).then_inc(rows_in[0][j], 16)
                    sp.dma_start(KB[:, j, :], a["dst"][bass.ds(g * GE, GE)].partition_broadcast(P)
                                 ).then_inc(rows_in[0][j], 16)

                with sp.Fori(0, PAIRS) as i:
                    rows0(i, 0)
                    rows0(i, 1)
                rows0(PAIRS, 0)

                for q in range(TG):
                    sp.wait_ge(scat[0][q], 16 * NG)
                for q in range(TG):
                    sp.dma_start(sm[:, q], sum0[q][0:N, :].rearrange(nodes, p=P)).then_inc(sums_in, 16)

            for b in range(NB):
                done_dve(sp, ("u", b))
                sp.dma_start(tZrow[b * P:(b + 1) * P, :], zrow[:, b % 2, :]).then_inc(z_out[b % 2], 16)
            sp.dma_start(tU.rearrange(nodes, p=P), urow[:]).then_inc(table_out, 16)
            sp.dma_start(tV.rearrange(nodes, p=P), vrow[:]).then_inc(table_out, 16)

            flag_ = load_flag(sp)
            with sp.If(flag_):
                def rows1w(t, j):
                    g = RB * t + j
                    done(sp, u_OT, t, j, RB)
                    sp.dma_start(KBT[:, j, :], a["dst"][bass.ds(g * GE, GE)].partition_broadcast(WG)
                                 ).then_inc(kbt_load[1][j], 16)
                    done(sp, u_S, t, j, RB)
                    sp.dma_start(KB[:, j, :], a["src"][bass.ds(g * GE, GE)].partition_broadcast(P)
                                 ).then_inc(kb_load[1][j], 16)
                    done(sp, u_V, t, j, RB)
                    sp.sem_inc(sp_go, 1)
                    first = sp.value_load(base_gi[0:1, bass.ds(g, 1)], min_val=0, max_val=N - WG)
                    sp.dma_start(VW[:, j, :], tV[bass.ds(first, WG), :]).then_inc(bw_load[j], 16)
                    done(sp, u_C, t, j, RB)
                    sp.sem_inc(sp_go, 1)
                    for q in range(TG):
                        first = sp.value_load(base_ti[0:1, bass.ds(g * TG + q, 1)], min_val=0, max_val=N - WT)
                        sp.dma_start(ZW[:, j, q, :], tZ[bass.ds(first * M, WT * M), :]).then_inc(zw_load[j], 16)

                sp.wait_ge(table_out, 64)
                sp.wait_ge(z_out[0], 16 * (NB - NB // 2))
                sp.wait_ge(z_out[1], 16 * (NB // 2))
                over_groups(sp, lambda t, j: back(rows1w, t, j, 0))
            with sp.Else():
                def rows1(i, j):
                    g = 2 * i + j
                    sp.wait_ge(dve_g[1], g * DVE1 + D1_S)
                    sp.dma_start(KB[:, j, :], a["src"][bass.ds(g * GE, GE)].partition_broadcast(P)
                                 ).then_inc(rows_in[1][j], 16)

                with sp.Fori(0, PAIRS) as i:
                    rows1(i, 0)
                    rows1(i, 1)
                rows1(PAIRS, 0)

            for q in range(TG):
                sp.wait_ge(scat[1][q], 16 * NG)
            for q in range(TG):
                sp.dma_start(sm[:, q, :, 0:D], sum1[q][0:N, :].rearrange(nodes, p=P)).then_inc(sums1_in, 16)
            done_dve(sp, "y")
            sp.dma_start(out.rearrange(nodes, p=P), h[:]).then_inc(y_out, 16)
            sp.wait_ge(y_out, 16)

        @block.gpsimd
        def _(pool):
            pool.memset(w_ab[:], 0.0)
            pool.memset(w_u[:], 0.0)
            pool.memset(zero, 0.0).then_inc(pool_memset, 1)
            pool.memset(ident[:], 0.0).then_inc(const_ready, 1)
            pool.wait_ge(const_ready, 1)
            pool.affine_select(out=ident[:], in_=ident[:], compare_op=ALU.not_equal, fill=1.0, base=0,
                               pattern=[[-1, 128]], channel_multiplier=1).then_inc(const_ready, 1)
            pool.wait_ge(const_ready, 2)
            pool.memset(tri[:], 1.0).then_inc(const_ready, 1)
            pool.wait_ge(const_ready, 3)
            pool.affine_select(out=tri[:], in_=tri[:], compare_op=ALU.is_gt, fill=0.0, base=0,
                               pattern=[[-1, P]], channel_multiplier=1).then_inc(const_ready, 1)
            pool.iota(trash[:], [[0, 1]], base=TRASH, channel_multiplier=1,
                      allow_small_or_imprecise_dtypes=True).then_inc(const_ready, 1)

            pool.iota(part[:], [[0, 1]], base=0, channel_multiplier=1,
                      allow_small_or_imprecise_dtypes=True).then_inc(const_ready, 1)
            pool.iota(iota_g[:], [[1, WG]], base=0, channel_multiplier=0,
                      allow_small_or_imprecise_dtypes=True).then_inc(const_ready, 1)

            def gathers0w(t, j):
                done(pool, slots_ready[0], t, j)
                pool.sem_inc(pool_go, 1)
                for q in range(TG):
                    pool.indirect_dma_start(X[0:P, j, q, D:2 * D], None, tA,
                                            bass.IndirectOffsetOnAxis(ap=slot_s[:, j, q:q + 1], axis=0)
                                            ).then_inc(gat_a[0][j][q], 16)

            def gathers1w(t, j):
                done(pool, slots_ready[1], t, j)
                pool.sem_inc(pool_go, 1)
                for q in range(TG):
                    pool.indirect_dma_start(U[:, j, q, :], None, tU,
                                            bass.IndirectOffsetOnAxis(ap=slot_s[:, j, q:q + 1], axis=0)
                                            ).then_inc(gat_a[1][j][q], 16)

            def scatters1w(t, j):
                for q in range(TG):
                    pool.wait_ge(scat[1][q], 16 * (RB * t + j))
                    pool.sem_inc(retired[1], 1)
                done(pool, u_CS, t, j)
                pool.sem_inc(pool_go, 1)
                for q in range(TG):
                    pool.indirect_dma_start(sum1[q], bass.IndirectOffsetOnAxis(ap=slot_c[:, j, q:q + 1], axis=0),
                                            C1[:, j, q, :], None, compute_op=ALU.add).then_inc(scat[1][q], 16)

            def body1w(t, j):
                back(gathers1w, t, j, 0)
                back(scatters1w, t, j, 4)

            def gathers(l, i, j):
                g = 2 * i + j
                pool.wait_ge(slots_ready[l], g + 1)
                pool.sem_inc(pool_go, 1)
                for q in range(TG):
                    to_a = X[0:P, j, q, D:2 * D] if l == 0 else U[:, j, q, :]
                    to_b = Y[:, j, q, :] if l == 0 else Z[:, j, q, :]
                    pool.indirect_dma_start(to_a, None, tA if l == 0 else tU,
                                            bass.IndirectOffsetOnAxis(ap=slot_s[:, j, q:q + 1], axis=0)
                                            ).then_inc(gat_a[l][j][q], 16)
                    pool.indirect_dma_start(to_b, None, tB if l == 0 else tZrow,
                                            bass.IndirectOffsetOnAxis(ap=slot_d[:, j, q:q + 1], axis=0)
                                            ).then_inc(gat_b[l][j][q], 16)
                    if l == 1:
                        pool.indirect_dma_start(V[:, j, q, :], None, tV,
                                                bass.IndirectOffsetOnAxis(ap=slot_d[:, j, q:q + 1], axis=0)
                                                ).then_inc(gat_v[j][q], 16)

            def scatters(l, i, j):
                g = 2 * i + j
                for q in range(TG):
                    pool.wait_ge(scat[l][q], 16 * g)
                    pool.sem_inc(retired[l], 1)
                pool.wait_ge(dve_g[l], g * (DVE0, DVE1)[l] + (D0_C, D1_C)[l] + 2 * (DVE0, DVE1)[l])
                pool.sem_inc(pool_go, 1)
                for q in range(TG):
                    pool.indirect_dma_start((sum0, sum1)[l][q],
                                            bass.IndirectOffsetOnAxis(ap=slot_c[:, j, q:q + 1], axis=0),
                                            (C, C1)[l][:, j, q, :], None, compute_op=ALU.add
                                            ).then_inc(scat[l][q], 16)

            for l in range(2):
                if l == 0:
                    pool.wait_ge(table_out, 32)
                    pool.wait_ge(zero_out, 16 * 2 * TG)
                else:
                    pool.wait_ge(table_out, 64)
                    pool.wait_ge(z_out[0], 16 * (NB - NB // 2))
                    pool.wait_ge(z_out[1], 16 * (NB // 2))
                flag_ = load_flag(pool)
                with pool.If(flag_):
                    if l == 0:
                        over_groups(pool, lambda t, j: back(gathers0w, t, j, 0))
                    else:
                        over_groups(pool, body1w)
                with pool.Else():
                    gathers(l, 0, 0)
                    with pool.Fori(0, PAIRS) as i:
                        gathers(l, i, 1)
                        scatters(l, i, 0)
                        gathers(l, i + 1, 0)
                        scatters(l, i, 1)
                    scatters(l, PAIRS, 0)

        @block.scalar
        def _(act):
            def norm_std(name, var):
                done_dve(act, var)
                act.activation(st[:, 2], st[:, 1], ACT.Sqrt, bias=eps_col[:, 0:1], scale=1.0 / D).then_inc(act_step, 1)

            def slots(l, i, j):
                g = 2 * i + j
                act.copy(slot_s[:, j, :], src_i[:, bass.ds(g * TG, TG)])
                act.copy(slot_d[:, j, :], dst_i[:, bass.ds(g * TG, TG)]).then_inc(slots_ready[l], 1)

            norm_std("std", "var")
            for c in range(NCH):
                lo, hi = chunk_cols(c)
                done_pe(act, ("hT", c))
                act.copy(hT[0:D, lo:hi], bank[c % 2][0:D, 0:hi - lo]).then_inc(act_step, 1)

            def group0(i, j):
                g = 2 * i + j
                act.wait_ge(pe_g[0], (g + 2) * PE0 + P0_T)
                act.copy(XT[:, j, :], bank[j % 2][:, 0:GE]).then_inc(act_g[0], 1)
                slots(0, i + 1, j)
                act.wait_ge(pe_g[0], (g + 2) * PE0 + P0_H1)
                act.activation(H1[0:D, j, :], bank[2 + j % 2][0:D, 0:GE], ACT.Relu).then_inc(act_g[0], 1)
                act.wait_ge(pe_g[0], (g + 2) * PE0 + P0_H2)
                act.activation(H2[:, j, :, 0:D], bank[4 + j % 2][0:P, 0:TG * D].rearrange("p (q f) -> p q f", q=TG),
                               ACT.Relu).then_inc(act_g[0], 1)

            done_dve(act, "padd")
            done_dve(act, ("turned_f", 5))
            act.sem_inc(act_g[0], 2 * ACT0)
            act.sem_inc(act_g[1], 2 * ACT1)

            def slots_w(l, t, j):
                act.copy(slot_s[:, j, :], src_i[:, bass.ds((RB * t + j) * TG, TG)]).then_inc(slots_ready[l], 1)

            def turned_w(t, j):
                done(act, f_T, t, j)
                done(act, f_h1, t, j, RB)
                act.copy(XT[:, j, :], bank[j % 2][:, 0:GE]).then_inc(f_XT, 1)
                slots_w(0, t + 1, j)

            def hidden1_w(t, j):
                done(act, f_h1, t, j)
                done(act, f_h2, t, j, RB)
                act.activation(H1[0:D, j, :], bank[2 + j % 2][0:D, 0:GE], ACT.Relu).then_inc(f_H1, 1)

            def hidden2_w(t, j):
                done(act, f_h2, t, j)
                done(act, f_seg, t, j, RB)
                act.activation(H2[:, j, :, 0:D], bank[4 + j % 2][0:P, 0:TG * D].rearrange("p (q f) -> p q f", q=TG),
                               ACT.Relu).then_inc(f_H2, 1)

            def body0w(t, j):
                back(turned_w, t, j, 0)
                back(hidden1_w, t, j, 1)
                back(hidden2_w, t, j, 2)

            flag_ = load_flag(act)
            with act.If(flag_):
                for j in range(RB):
                    slots_w(0, 0, j)
                over_groups(act, body0w)
            with act.Else():
                slots(0, 0, 0)
                slots(0, 0, 1)
                with act.Fori(0, PAIRS) as i:
                    group0(i, 0)
                    group0(i, 1)
                group0(PAIRS, 0)
                for c in range(NCH):
                    lo, hi = chunk_cols(c)
                    act.wait_ge(sum_pe, c + 1)
                    act.copy(sT[:, lo:hi], bank[c % 2][0:DC, 0:hi - lo]).then_inc(sum_act, 1)
                act.wait_ge(sum_act, NCH)
                act.sem_inc(sT_ready, 1)

            for s, to in (("g1", hT), ("g2", nT2)):
                for c in range(NCH):
                    lo, hi = chunk_cols(c)
                    done_pe(act, (s, c))
                    act.activation(to[0:D, lo:hi], bank[c % 2][0:D, 0:hi - lo], ACT.Relu).then_inc(act_step, 1)
            norm_std("std'", "var'")
            for c in range(NCH):
                lo, hi = chunk_cols(c)
                done_pe(act, ("h'T", c))
                act.copy(hT[0:D, lo:hi], bank[c % 2][0:D, 0:hi - lo]).then_inc(act_step, 1)

            def group1(i, j):
                g = 2 * i + j
                act.wait_ge(dve_g[1], (g + 2) * DVE1 + D1_SUB)
                act.activation(EX[:, j], L[:, j], ACT.Exp).then_inc(act_g[1], 1)
                act.wait_ge(pe_g[1], (g + 2) * PE1 + P1_C)
                slots(1, i + 1, j)

            def exps_w(t, j):
                done(act, u_L, t, j)
                done(act, u_Q, t, j, RB)
                act.activation(EX[:, j], L[:, j], ACT.Exp).then_inc(u_EX, 1)
                slots_w(1, t + 1, j)

            def reduced_w(t, j):
                done(act, u_R, t, j)
                done(act, u_C, t, j, RB)
                act.copy(R[:, j, :], bank[2 + j % 2][:, 0:GE]).then_inc(u_RS, 1)

            def combined_w(t, j):
                g = RB * t + j
                done(act, u_C, t, j)
                act.wait_ge(retired[1], TG * g)
                act.copy(slot_c[:, j, :], slot_all[:, bass.ds(g * TG, TG)])
                act.copy(C1[:, j], bank[4 + j % 2][0:P, 0:TG * D].rearrange("p (q f) -> p q f", q=TG)).then_inc(u_CS, 1)

            def body1w(t, j):
                back(reduced_w, t, j, 2)
                back(combined_w, t, j, 3)
                back(exps_w, t, j, 1)

            flag_ = load_flag(act)
            with act.If(flag_):
                act.wait_ge(f_dd, NG)
                for j in range(RB):
                    slots_w(1, 0, j)
                over_groups(act, body1w)
            with act.Else():
                slots(1, 0, 0)
                slots(1, 0, 1)
                with act.Fori(0, PAIRS) as i:
                    group1(i, 0)
                    group1(i, 1)
                group1(PAIRS, 0)

        @block.vector
        def _(dve):
            def step(ins):
                ins.then_inc(dve_step, 1)

            windows = [0]

            def win(ins):
                windows[0] += 1
                ins.then_inc(win_dve, 1)
                dve.wait_ge(win_dve, windows[0])

            def layer_norm(t):
                step(dve.tensor_reduce(st[:, 0], x[:], AX_X, ALU.add))
                done_dve(dve, "mean" + t)
                step(dve.scalar_tensor_tensor(out=h[:], in0=st[:, 0].unsqueeze(2).to_broadcast([P, NB, D]),
                                              scalar=-1.0 / D, in1=x[:], op0=ALU.mult, op1=ALU.add))
                done_dve(dve, "xc" + t)
                step(dve.tensor_tensor(sq, h[:], h[:], ALU.mult))
                done_dve(dve, "sq" + t)
                step(dve.tensor_reduce(st[:, 1], sq, AX_X, ALU.add))
                done_act(dve, "std" + t)
                step(dve.reciprocal(st[:, 3], st[:, 2]))
                done_dve(dve, "rstd" + t)
                step(dve.tensor_tensor(h[:], h[:], st[:, 3].unsqueeze(2).to_broadcast([P, NB, D]), ALU.mult))
                done_dve(dve, "norm" + t)
                step(dve.tensor_scalar(h[:], h[:], 0.0, None, ALU.max))

            dve.memset(eps_col[:], EPS)
            win(dve.memset(ones[:], 1.0))
            win(dve.memset(sT[:], 0.0))
            dve.wait_ge(idx_in, 48)
            step(dve.tensor_copy(raw[:, 0:2], rawi))
            step(dve.memset(hT[D:DC, :], 1.0))
            step(dve.memset(nT2[D:DC, :], 1.0))
            step(dve.memset(H1[D:DC, :, :], 1.0))
            step(dve.memset(H2[:, :, :, D:DC], 1.0))
            dve.wait_ge(weights_in, 16 * WL)
            step(dve.tensor_scalar(w_u[0:D, 0:M], w_u[0:D, M:2 * M], -1.0, None, ALU.mult))
            step(dve.memset(src_i[:, NT:], 0))
            step(dve.memset(dst_i[:, NT:], 0))
            dve.wait_ge(const_ready, 2)
            step(dve.tensor_copy(w_ex[D:2 * D, :], ident[D:2 * D, D:2 * D]))
            for k in range(6):
                what, half = k // 2, k % 2
                lo, hi = (0, 6 * IC) if half == 0 else (6 * IC, NT)
                done_pe(dve, ("turn", k))
                t = (src_i, dst_i, wgt)[what]
                tf = (src_f, dst_f, wgt)[what]
                step(dve.tensor_copy(t[:, lo:hi], bank[2 + k][0:P, 0:hi - lo]))
                if what == 2:
                    done_dve(dve, ("turned", k))
                step(dve.tensor_copy(tf[:, lo:hi], bank[2 + k][0:P, 0:hi - lo]))
            for k in range(2):
                lo, hi = (0, 6 * IC) if k == 0 else (6 * IC, NT)
                dve.wait_ge(win_pe, k + 1)
                win(dve.tensor_copy(base[:, lo:hi], bank[2 + k][0:P, 0:hi - lo]))
            win(dve.tensor_scalar(base_g[:], base[:, 0:NT:TG], float(N - WG), None, ALU.min))
            win(dve.tensor_scalar(base[:], base[:], float(N - WT), None, ALU.min))
            win(dve.tensor_copy(base_gi[:], base_g[0:1, :]))
            win(dve.tensor_copy(base_ti[:], base[0:1, :]))
            dve.wait_ge(const_ready, 6)
            win(dve.tensor_scalar(base_p[:], base_g[:], part[:, 0:1], None, ALU.add))
            win(dve.tensor_tensor(rel_g[:].rearrange("p (g q) -> p g q", q=TG),
                                  dst_f[:].rearrange("p (g q) -> p g q", q=TG),
                                  base_g[:].unsqueeze(2).to_broadcast([P, NG, TG]), ALU.subtract))
            win(dve.tensor_tensor(rel_t[:], dst_f[:], base[:], ALU.subtract))
            win(dve.tensor_reduce(span[:, 0:1], rel_g[:], AX_X, ALU.max))
            win(dve.tensor_reduce(span[:, 1:2], rel_g[:], AX_X, ALU.min))
            win(dve.tensor_reduce(span[:, 2:3], rel_t[:], AX_X, ALU.max))
            win(dve.tensor_reduce(span[:, 3:4], rel_t[:], AX_X, ALU.min))
            win(dve.tensor_scalar(span[:, 4:5], span[:, 0:1], float(1 - WG), None, ALU.add))
            win(dve.tensor_scalar(span[:, 5:6], span[:, 2:3], float(1 - WT), None, ALU.add))
            win(dve.tensor_scalar(span[:, 6:7], span[:, 1:2], -1.0, None, ALU.mult))
            win(dve.tensor_scalar(span[:, 7:8], span[:, 3:4], -1.0, None, ALU.mult))
            win(dve.tensor_reduce(span[:, 0:1], span[:, 4:8], AX_X, ALU.max))
            dve.wait_ge(win_pe, 3)
            win(dve.tensor_reduce(flag[:, 0:1], bank[4][0:1, 0:P], AX_X, ALU.max))
            win(dve.tensor_scalar(flag[:, 1:2], flag[:, 0:1], 0.0, None, ALU.is_le))
            dve.tensor_copy(flag_i[:], flag[:, 1:2]).then_inc(flag_ready, 1)

            dve.wait_ge(x_in, 16)
            layer_norm("")
            for c in range(NCH):
                b = chunk_blocks(c)
                done_pe(dve, ("ab", c))
                step(dve.tensor_copy(ab[:, b[0]:b[-1] + 1, :],
                                     bank[c % 2][0:P, 0:len(b) * 2 * D].rearrange("p (b f) -> p b f", f=2 * D)))

            dve.sem_inc(dve_g[0], 2 * DVE0)
            dve.sem_inc(dve_g[1], 2 * DVE1)
            dve.wait_ge(const_ready, 7)

            def equal_rows(l, i, j, keys):
                g = 2 * i + j
                base, s = (g + 2) * (DVE0, DVE1)[l], dve_g[l]
                kf = keys[:, bass.ds(g * TG, TG)]
                dve.wait_ge(rows_in[l][j], (i + 1) * (32, 16)[l])
                dve.wait_ge(pe_g[l], (g + 1) * (PE0, PE1)[l])
                dve.tensor_tensor(S[:, j], KB[:, j, :].rearrange("p (q f) -> p q f", q=TG),
                                  kf.unsqueeze(2).to_broadcast([P, TG, P]), ALU.is_equal).then_inc(s, 1)
                dve.wait_ge(s, base + D0_S)
                dve.tensor_tensor(SL[:], S[:, j], tri[:].unsqueeze(1).to_broadcast([P, TG, P]),
                                  ALU.mult).then_inc(s, 1)
                dve.wait_ge(s, base + D0_SL)
                dve.tensor_reduce(dd[:, 0], SL[:], AX_X, ALU.add).then_inc(s, 1)
                dve.wait_ge(s, base + D0_CNT)
                dve.tensor_scalar(dd[:, 1], dd[:, 0], 1.0, None, ALU.min).then_inc(s, 1)
                dve.tensor_scalar(dd[:, 2], kf, -1.0, trash[:, 0:1], ALU.mult, ALU.add).then_inc(s, 1)
                dve.wait_ge(s, base + D0_OFF)
                dve.tensor_tensor(dd[:, 3], dd[:, 1], dd[:, 2], ALU.mult).then_inc(s, 1)
                dve.wait_ge(s, base + D0_MUL)
                dve.wait_ge(retired[l], TG * g)
                dve.tensor_tensor(slot_c[:, j, :], dd[:, 3], kf, ALU.add).then_inc(s, 1)

            def group0(i, j):
                g = 2 * i + j
                base = (g + 2) * DVE0
                equal_rows(0, i, j, dst_f)
                for q in range(TG):
                    dve.wait_ge(gat_a[0][j][q], (i + 1) * 16)
                    dve.wait_ge(gat_b[0][j][q], (i + 1) * 16)
                dve.tensor_tensor(X[0:P, j, :, D:2 * D], X[0:P, j, :, D:2 * D], Y[:, j], ALU.add).then_inc(dve_g[0], 1)
                dve.wait_ge(pe_g[0], (g + 2) * PE0 + P0_C)
                dve.tensor_copy(C[:, j], bank[6 + j % 2][0:P, 0:TG * DC].rearrange("p (q f) -> p q f", q=TG)
                                ).then_inc(dve_g[0], 1)

            def window_t(t, j):
                dve.wait_ge(kbt_load[0][j], (t + 1) * 16)
                done(dve, f_h1, t, j, RB)
                dve.tensor_scalar(OT[:, j, :], KBT[:, j, :], base_p[0:WG, bass.ds(RB * t + j, 1)], None,
                                  ALU.is_equal).then_inc(f_OT, 1)

            def window_e(t, j):
                done(dve, f_seg, t, j, RB)
                dve.tensor_tensor(OE[:, j], iota_g[:].unsqueeze(1).to_broadcast([P, TG, WG]),
                                  rel_g[:, bass.ds((RB * t + j) * TG, TG)].unsqueeze(2).to_broadcast([P, TG, WG]),
                                  ALU.is_equal).then_inc(f_OE, 1)

            def add_window(t, j):
                done(dve, f_seg, t, j)
                done(dve, f_acc, t, j, 1)
                first = dve.value_load(base_gi[0:1, bass.ds(RB * t + j, 1)], min_val=0, max_val=N - WG)
                to = sT[:, bass.ds(first, WG)]
                dve.tensor_tensor(to, to, bank[6 + j % 2][0:DC, 0:WG], ALU.add).then_inc(f_acc, 1)

            DDN = 7

            def first_edges(t, j):
                g = RB * t + j
                kf = src_f[:, bass.ds(g * TG, TG)]
                dve.wait_ge(kb_load[0][j], (t + 1) * 16)
                dve.tensor_tensor(SL[:], KB[:, j, :].rearrange("p (q f) -> p q f", q=TG),
                                  kf.unsqueeze(2).to_broadcast([P, TG, P]), ALU.is_equal).then_inc(f_chain, 1)
                dve.wait_ge(f_chain, g * DDN + 1)
                dve.tensor_tensor(SL[:], SL[:], tri[:].unsqueeze(1).to_broadcast([P, TG, P]),
                                  ALU.mult).then_inc(f_chain, 1)
                dve.wait_ge(f_chain, g * DDN + 2)
                dve.tensor_reduce(dd[:, 0], SL[:], AX_X, ALU.add).then_inc(f_chain, 1)
                dve.wait_ge(f_chain, g * DDN + 3)
                dve.tensor_scalar(dd[:, 1], dd[:, 0], 1.0, None, ALU.min).then_inc(f_chain, 1)
                dve.tensor_scalar(dd[:, 2], kf, -1.0, trash[:, 0:1], ALU.mult, ALU.add).then_inc(f_chain, 1)
                dve.wait_ge(f_chain, g * DDN + 5)
                dve.tensor_tensor(dd[:, 3], dd[:, 1], dd[:, 2], ALU.mult).then_inc(f_chain, 1)
                dve.wait_ge(f_chain, g * DDN + 6)
                dve.tensor_tensor(slot_all[:, bass.ds(g * TG, TG)], dd[:, 3], kf, ALU.add).then_inc(f_chain, 1)
                dve.wait_ge(f_chain, g * DDN + 7)
                dve.sem_inc(f_dd, 1)

            def body0w(t, j):
                back(window_t, t, j, 0)
                back(first_edges, t, j, 1)
                back(window_e, t, j, 2)
                back(add_window, t, j, 3)

            flag_ = load_flag(dve)
            with dve.If(flag_):
                over_groups(dve, body0w)
                dve.wait_ge(f_acc, NG)
                dve.sem_inc(sT_ready, 1)
            with dve.Else():
                with dve.Fori(0, PAIRS) as i:
                    group0(i, 0)
                    group0(i, 1)
                group0(PAIRS, 0)
                dve.wait_ge(sums_in, 16 * TG)
                dve.tensor_tensor(sm[:, 0], sm[:, 0], sm[:, 1], ALU.add).then_inc(sum_dve, 1)
                dve.wait_ge(sum_dve, 1)
                dve.tensor_tensor(sm[:, 0], sm[:, 0], sm[:, 2], ALU.add).then_inc(sum_dve, 1)

            for c in range(NCH):
                lo, hi = chunk_cols(c)
                done_pe(dve, ("agg", c))
                step(dve.tensor_copy(nT2[0:D, lo:hi], bank[2 + c % 2][0:D, 0:hi - lo]))
            for c in range(NCH):
                b = chunk_blocks(c)
                done_pe(dve, ("x1", c))
                step(dve.tensor_tensor(x[:, b[0]:b[-1] + 1, :], x[:, b[0]:b[-1] + 1, :],
                                       bank[4 + c % 2][0:P, 0:len(b) * D].rearrange("p (b f) -> p b f", f=D), ALU.add))
            done_dve(dve, ("x1", NCH - 1))
            layer_norm("'")
            for b in range(NB):
                done_pe(dve, ("z", b))
                if b >= 2:
                    dve.wait_ge(z_out[b % 2], 16 * (b // 2))
                step(dve.tensor_copy(zrow[:, b % 2, 0:M * D], bank[2 * (b % 2)][0:P, :]))
                dve.tensor_copy(urow[:, b, :], bank[2 * (b % 2) + 1][0:P, M:2 * M])
                step(dve.tensor_copy(vrow[:, b, :], bank[2 * (b % 2) + 1][0:P, 0:M]))

            def group1(i, j):
                g = 2 * i + j
                base, s = (g + 2) * DVE1, dve_g[1]
                equal_rows(1, i, j, src_f)
                for q in range(TG):
                    dve.wait_ge(gat_a[1][j][q], (i + 1) * 16)
                    dve.wait_ge(gat_b[1][j][q], (i + 1) * 16)
                    dve.wait_ge(gat_v[j][q], (i + 1) * 16)
                dve.tensor_tensor(L[:, j], U[:, j], V[:, j], ALU.add).then_inc(s, 1)
                dve.wait_ge(s, base + D1_LOG)
                dve.tensor_reduce(r4[:, 0], L[:, j], AX_X, ALU.max).then_inc(s, 1)
                dve.wait_ge(s, base + D1_MAX)
                dve.tensor_tensor(L[:, j], L[:, j], r4[:, 0].unsqueeze(2).to_broadcast([P, TG, M]),
                                  ALU.subtract).then_inc(s, 1)
                dve.wait_ge(act_g[1], (g + 2) * ACT1 + A1_EXP)
                dve.tensor_reduce(r4[:, 1], EX[:, j], AX_X, ALU.add).then_inc(s, 1)
                dve.wait_ge(s, base + D1_SUM)
                dve.reciprocal(r4[:, 2], r4[:, 1]).then_inc(s, 1)
                dve.wait_ge(s, base + D1_REC)
                dve.tensor_tensor(r4[:, 3], r4[:, 2], wgt[:, bass.ds(g * TG, TG)], ALU.mult).then_inc(s, 1)
                dve.wait_ge(s, base + D1_QS)
                dve.tensor_tensor(EX[:, j], EX[:, j], r4[:, 3].unsqueeze(2).to_broadcast([P, TG, M]),
                                  ALU.mult).then_inc(s, 1)
                dve.wait_ge(s, base + D1_QW)
                for q in range(TG):
                    zq = Z[:, j, q, 0:M * D].rearrange("p (m f) -> p m f", m=M)
                    last = dve.tensor_tensor(zq, zq, EX[:, j, q].unsqueeze(2).to_broadcast([P, M, D]), ALU.mult)
                last.then_inc(s, 1)
                dve.wait_ge(pe_g[1], (g + 2) * PE1 + P1_C)
                dve.tensor_copy(C1[:, j], bank[6 + j % 2][0:P, 0:TG * D].rearrange("p (q f) -> p q f", q=TG)
                                ).then_inc(s, 1)

            def window1_t(t, j):
                dve.wait_ge(kbt_load[1][j], (t + 1) * 16)
                done(dve, u_V, t, j, RB)
                dve.tensor_scalar(OT[:, j, :], KBT[:, j, :], base_p[0:WG, bass.ds(RB * t + j, 1)], None,
                                  ALU.is_equal).then_inc(u_OT, 1)

            def logits_w(t, j):
                g = RB * t + j
                kf = src_f[:, bass.ds(g * TG, TG)]
                dve.wait_ge(kb_load[1][j], (t + 1) * 16)
                done(dve, u_R, t, j, RB)
                dve.tensor_tensor(S[:, j], KB[:, j, :].rearrange("p (q f) -> p q f", q=TG),
                                  kf.unsqueeze(2).to_broadcast([P, TG, P]), ALU.is_equal).then_inc(u_S, 1)
                for q in range(TG):
                    dve.wait_ge(gat_a[1][j][q], (t + 1) * 16)
                done(dve, u_V, t, j)
                done(dve, u_EX, t, j, RB)
                dve.tensor_tensor(L[:, j], U[:, j], bank[j % 2][0:P, 0:TG * M].rearrange("p (q m) -> p q m", q=TG),
                                  ALU.add).then_inc(u_chain, 1)
                dve.wait_ge(u_chain, chain1(t, j, 0))
                dve.tensor_reduce(r4[:, 0], L[:, j], AX_X, ALU.max).then_inc(u_chain, 1)
                dve.wait_ge(u_chain, chain1(t, j, 1))
                dve.tensor_tensor(L[:, j], L[:, j], r4[:, 0].unsqueeze(2).to_broadcast([P, TG, M]),
                                  ALU.subtract).then_inc(u_L, 1)

            def weights_w(t, j):
                g = RB * t + j
                done(dve, u_EX, t, j)
                dve.tensor_reduce(r4[:, 1], EX[:, j], AX_X, ALU.add).then_inc(u_chain2, 1)
                dve.tensor_tensor(OH[:, j], iota_g[:, 0:WT].unsqueeze(1).to_broadcast([P, TG, WT]),
                                  rel_t[:, bass.ds(g * TG, TG)].unsqueeze(2).to_broadcast([P, TG, WT]),
                                  ALU.is_equal).then_inc(u_chain2, 1)
                dve.wait_ge(u_chain2, g * 5 + 2)
                dve.reciprocal(r4[:, 2], r4[:, 1]).then_inc(u_chain2, 1)
                dve.wait_ge(u_chain2, g * 5 + 3)
                dve.tensor_tensor(r4[:, 3], r4[:, 2], wgt[:, bass.ds(g * TG, TG)], ALU.mult).then_inc(u_chain2, 1)
                dve.wait_ge(u_chain2, g * 5 + 4)
                dve.tensor_tensor(EX[:, j], EX[:, j], r4[:, 3].unsqueeze(2).to_broadcast([P, TG, M]),
                                  ALU.mult).then_inc(u_chain2, 1)
                dve.wait_ge(u_chain2, g * 5 + 5)
                done(dve, u_R, t, j, RB)
                dve.tensor_tensor(Q[:, j], OH[:, j].unsqueeze(3).to_broadcast([P, TG, WT, M]),
                                  EX[:, j].unsqueeze(2).to_broadcast([P, TG, WT, M]), ALU.mult).then_inc(u_Q, 1)

            def chain1(t, j, k):
                return (RB * t + j) * 2 + k + 1

            def body1w(t, j):
                back(weights_w, t, j, 2)
                back(logits_w, t, j, 1)
                back(window1_t, t, j, 0)

            flag_ = load_flag(dve)
            with dve.If(flag_):
                over_groups(dve, body1w)
            with dve.Else():
                with dve.Fori(0, PAIRS) as i:
                    group1(i, 0)
                    group1(i, 1)
                group1(PAIRS, 0)

            dve.wait_ge(sums1_in, 16 * TG)
            step(dve.tensor_tensor(h[:], sm[:, 0, :, 0:D], sm[:, 1, :, 0:D], ALU.add))
            done_dve(dve, "y01")
            step(dve.tensor_tensor(h[:], h[:], sm[:, 2, :, 0:D], ALU.add))
            done_dve(dve, "y012")
            step(dve.tensor_tensor(h[:], h[:], vb[:].unsqueeze(1).to_broadcast([P, NB, D]), ALU.add))
            done_dve(dve, "yx")
            step(dve.tensor_tensor(h[:], h[:], x[:], ALU.add))

        @block.tensor
        def _(pe):
            def turn_nodes(name, from_, width, act_name):
                for c in range(NCH):
                    if c >= 2:
                        done_act(pe, (act_name, c - 2))
                    for n, b in enumerate(chunk_blocks(c)):
                        last = pe.transpose(bank[c % 2][0:width, n * P:(n + 1) * P], from_(b), ident[0:P, 0:P])
                    last.then_inc(pe_step, 1)

            pe.wait_ge(const_ready, 2)
            done_dve(pe, "rawf")
            for k in range(6):
                what, half = k // 2, k % 2
                for n, c in enumerate(range(0, 6) if half == 0 else range(6, NIC)):
                    last = pe.transpose(bank[2 + k][0:P, n * IC:(n + 1) * IC], raw[:, what, c, :], ident[0:IC, 0:IC])
                last.then_inc(pe_step, 1)

            done_dve(pe, ("turned_f", 5))
            pe.wait_ge(win_dve, 1)
            for k in range(2):
                lo, hi = (0, 6 * IC) if k == 0 else (6 * IC, NT)
                pe.matmul(bank[2 + k][0:P, 0:hi - lo], ones[:], dst_f[0:1, lo:hi], start=True, stop=True
                          ).then_inc(win_pe, 1)
            pe.wait_ge(win_dve, WIN_SPAN)
            pe.transpose(bank[4][0:1, 0:P], span[:, 0:1], ident[0:P, 0:P]).then_inc(win_pe, 1)

            done_dve(pe, "relu")
            turn_nodes("hT", lambda b: h[:, b, :], D, "hT")
            done_act(pe, ("hT", NCH - 1))
            for c in range(NCH):
                if c >= 2:
                    done_dve(pe, ("ab", c - 2))
                for n, b in enumerate(chunk_blocks(c)):
                    last = pe.matmul(bank[c % 2][0:P, n * 2 * D:(n + 1) * 2 * D], hT[:, b * P:(b + 1) * P], w_ab[:],
                                     start=True, stop=True)
                last.then_inc(pe_step, 1)
            done_dve(pe, ("ab", NCH - 1))

            pe.sem_inc(pe_g[0], 2 * PE0)
            pe.sem_inc(pe_g[1], 2 * PE1)

            def group0(i, j):
                g = 2 * i + j
                pe.wait_ge(rows_in[0][j], (i + 1) * 32)
                pe.wait_ge(dve_g[0], (g + 2) * DVE0 + D0_SUM)
                for q in range(TG):
                    last = pe.transpose(bank[j % 2][:, q * P:(q + 1) * P], X[0:P, j, q, :], ident[0:P, 0:P])
                last.then_inc(pe_g[0], 1)
                pe.wait_ge(act_g[0], (g + 2) * ACT0 + A0_XT)
                pe.matmul(bank[2 + j % 2][0:D, 0:GE], w_ex[:], XT[:, j, :], start=True, stop=True).then_inc(pe_g[0], 1)
                pe.wait_ge(act_g[0], (g + 2) * ACT0 + A0_H1)
                for q in range(TG):
                    last = pe.matmul(bank[4 + j % 2][0:P, q * D:(q + 1) * D], H1[:, j, q * P:(q + 1) * P], w2[:],
                                     start=True, stop=True)
                last.then_inc(pe_g[0], 1)
                pe.wait_ge(act_g[0], (g + 2) * ACT0 + A0_H2)
                for q in range(TG):
                    last = pe.matmul(bank[6 + j % 2][0:P, q * DC:(q + 1) * DC], S[:, j, q, :], H2[:, j, q, :],
                                     start=True, stop=True)
                last.then_inc(pe_g[0], 1)

            def turn_w(t, j):
                pe.wait_ge(x_load[j], (t + 1) * 16)
                for q in range(TG):
                    pe.wait_ge(gat_a[0][j][q], (t + 1) * 16)
                done(pe, f_XT, t, j, 2)
                for q in range(TG):
                    last = pe.transpose(bank[j % 2][:, q * P:(q + 1) * P], X[0:P, j, q, :], ident[0:P, 0:P])
                last.then_inc(f_T, 1)

            def layer1_w(t, j):
                done(pe, f_OT, t, j)
                pe.wait_ge(bw_load[j], (t + 1) * 16)
                done(pe, f_XT, t, j)
                done(pe, f_H1, t, j, 2)
                pe.matmul(bank[2 + j % 2][0:D, 0:GE], w_ex[:], XT[:, j, :], start=True, stop=False)
                pe.matmul(bank[2 + j % 2][0:D, 0:GE], BW[:, j, :], OT[:, j, :], start=False, stop=True
                          ).then_inc(f_h1, 1)

            def layer2_w(t, j):
                done(pe, f_H1, t, j)
                done(pe, f_H2, t, j, 2)
                for q in range(TG):
                    last = pe.matmul(bank[4 + j % 2][0:P, q * D:(q + 1) * D], H1[:, j, q * P:(q + 1) * P], w2[:],
                                     start=True, stop=True)
                last.then_inc(f_h2, 1)

            def segment_w(t, j):
                done(pe, f_H2, t, j)
                done(pe, f_OE, t, j)
                done(pe, f_acc, t, j, 2)
                for q in range(TG):
                    last = pe.matmul(bank[6 + j % 2][0:DC, 0:WG], H2[:, j, q, :], OE[:, j, q, :],
                                     start=(q == 0), stop=(q == TG - 1))
                last.then_inc(f_seg, 1)

            def body0w(t, j):
                back(turn_w, t, j, 0)
                back(layer1_w, t, j, 1)
                back(layer2_w, t, j, 2)
                back(segment_w, t, j, 3)

            flag_ = load_flag(pe)
            with pe.If(flag_):
                over_groups(pe, body0w)
            with pe.Else():
                with pe.Fori(0, PAIRS) as i:
                    group0(i, 0)
                    group0(i, 1)
                group0(PAIRS, 0)
                pe.wait_ge(sum_dve, 2)
                for c in range(NCH):
                    if c >= 2:
                        pe.wait_ge(sum_act, c - 1)
                    for n, b in enumerate(chunk_blocks(c)):
                        last = pe.transpose(bank[c % 2][0:DC, n * P:(n + 1) * P], sm[:, 0, b, :], ident[0:P, 0:P])
                    last.then_inc(sum_pe, 1)

            pe.wait_ge(sT_ready, 1)
            for c in range(NCH):
                lo, hi = chunk_cols(c)
                if c >= 2:
                    done_dve(pe, ("agg", c - 2))
                pe.matmul(bank[2 + c % 2][0:D, 0:hi - lo], w3[:], sT[:, lo:hi], start=True, stop=True
                          ).then_inc(pe_step, 1)
            done_dve(pe, ("agg", NCH - 1))
            for c in range(NCH):
                lo, hi = chunk_cols(c)
                if c >= 2:
                    done_act(pe, ("g1", c - 2))
                pe.matmul(bank[c % 2][0:D, 0:hi - lo], wn1h[:], hT[:, lo:hi], start=True, stop=False)
                pe.matmul(bank[c % 2][0:D, 0:hi - lo], wn1a[:], nT2[0:D, lo:hi], start=False, stop=True
                          ).then_inc(pe_step, 1)
            done_act(pe, ("g1", NCH - 1))
            for c in range(NCH):
                lo, hi = chunk_cols(c)
                if c >= 2:
                    done_act(pe, ("g2", c - 2))
                pe.matmul(bank[c % 2][0:D, 0:hi - lo], wn2[:], hT[:, lo:hi], start=True, stop=True
                          ).then_inc(pe_step, 1)
            done_act(pe, ("g2", NCH - 1))
            for c in range(NCH):
                if c >= 2:
                    done_dve(pe, ("x1", c - 2))
                for n, b in enumerate(chunk_blocks(c)):
                    last = pe.matmul(bank[4 + c % 2][0:P, n * D:(n + 1) * D], nT2[:, b * P:(b + 1) * P], wn3[:],
                                     start=True, stop=True)
                last.then_inc(pe_step, 1)
            done_dve(pe, "relu'")
            turn_nodes("h'T", lambda b: h[:, b, :], D, "h'T")
            done_act(pe, ("h'T", NCH - 1))
            for b in range(NB):
                if b >= 2:
                    done_dve(pe, ("u", b - 2))
                pe.matmul(bank[2 * (b % 2)][0:P, :], hT[0:D, b * P:(b + 1) * P],
                          w_z[:].rearrange("c m d -> c (m d)"), start=True, stop=True)
                pe.matmul(bank[2 * (b % 2) + 1][0:P, 0:2 * M], hT[:, b * P:(b + 1) * P], w_u[:],
                          start=True, stop=True).then_inc(pe_step, 1)
            done_dve(pe, ("u", NB - 1))

            def group1(i, j):
                g = 2 * i + j
                pe.wait_ge(dve_g[1], (g + 2) * DVE1 + D1_Z)
                for q in range(TG):
                    for m in range(M):
                        last = pe.matmul(bank[6 + j % 2][0:P, q * D:(q + 1) * D], S[:, j, q, :],
                                         Z[:, j, q, m * D:(m + 1) * D], start=(m == 0), stop=(m == M - 1))
                last.then_inc(pe_g[1], 1)

            def logits_w(t, j):
                done(pe, u_OT, t, j)
                pe.wait_ge(bw_load[j], (NG - j + RB - 1) // RB * 16 + (t + 1) * 16)
                done(pe, u_L, t, j, 2)
                for q in range(TG):
                    last = pe.matmul(bank[j % 2][0:P, q * M:(q + 1) * M], OT[:, j, q * P:(q + 1) * P], VW[:, j, :],
                                     start=True, stop=True)
                last.then_inc(u_V, 1)

            def reduce_w(t, j):
                done(pe, u_Q, t, j)
                done(pe, u_S, t, j)
                done(pe, u_RS, t, j, 2)
                for q in range(TG):
                    last = pe.matmul(bank[2 + j % 2][:, q * P:(q + 1) * P], Q[:, j, q].rearrange("p n m -> p (n m)"),
                                     S[:, j, q, :], start=True, stop=True)
                last.then_inc(u_R, 1)

            def combine_w(t, j):
                done(pe, u_RS, t, j)
                pe.wait_ge(zw_load[j], (t + 1) * 16 * TG)
                done(pe, u_CS, t, j, 2)
                for q in range(TG):
                    last = pe.matmul(bank[4 + j % 2][0:P, q * D:(q + 1) * D], R[:, j, q * P:(q + 1) * P],
                                     ZW[:, j, q, :], start=True, stop=True)
                last.then_inc(u_C, 1)

            def body1w(t, j):
                back(reduce_w, t, j, 2)
                back(combine_w, t, j, 3)
                back(logits_w, t, j, 0)

            flag_ = load_flag(pe)
            with pe.If(flag_):
                over_groups(pe, body1w)
            with pe.Else():
                with pe.Fori(0, PAIRS) as i:
                    group1(i, 0)
                    group1(i, 1)
                group1(PAIRS, 0)


NAMES = ["x", "src", "dst", "edge_attr_64", "edge_weight", "L0_gnn_We1", "L0_gnn_be1", "L0_gnn_We2", "L0_gnn_be2",
         "L0_gnn_We3", "L0_gnn_be3", "L0_gnn_Wn1", "L0_gnn_bn1", "L0_gnn_Wn2", "L0_gnn_bn2", "L0_gnn_Wn3",
         "L0_gnn_bn3", "L1_gnn_var_u", "L1_gnn_var_c", "L1_gnn_var_w", "L1_gnn_var_b"]


def kernel(**inputs):
    import numpy as _np
    import concourse.bacc as _bacc
    from concourse import mybir as _mybir
    from concourse.bass_utils import run_bass_kernel_spmd as _run

    nc = _bacc.Bacc("TRN2", target_bir_lowering=False, num_devices=1)
    arrays, aps = {}, {}
    for name in NAMES:
        v = _np.ascontiguousarray(inputs[name])
        arrays[f"in_{name}"] = v
        aps[name] = nc.dram_tensor(f"in_{name}", v.shape, _mybir.dt.from_np(v.dtype), kind="ExternalInput").ap()
    out = nc.dram_tensor("out_0", (N, D), _mybir.dt.float32, kind="ExternalOutput").ap()
    build_gnn(nc, aps, out)
    r = _run(nc, [arrays], core_ids=[0])
    return r.results[0]["out_0"]
```

```python
from contextlib import ExitStack

import concourse.bass as bass
from concourse import mybir

F32 = mybir.dt.float32
I32 = mybir.dt.int32
BF16 = mybir.dt.bfloat16
I16 = mybir.dt.int16
ALU = mybir.AluOpType
ACT = mybir.ActivationFunctionType
AX_X = mybir.AxisListType.X

N = 3125
E = 103125
D = 64
M = 8
P = 125
NB = N // P
NT = E // P
TG = 3
NG = NT // TG
GE = TG * P
PAIRS = NG // 2
TRASH = N
ROWS = N + P
IC = 75
NIC = NT // IC
DC = D + 1
ZC = M * D
RB = 4
TURNS = NG // RB
WG = 64
WT = 16
CB = 4
NCH = -(-NB // CB)
CW = CB * P
EPS = 1e-5
ROUND = 1.5 * 2.0 ** 23
ZBACK = 3
PARTS = 3
TW = 256


def chunk_blocks(c):
    return range(c * CB, min(NB, c * CB + CB))


def chunk_cols(c):
    return c * CW, min(N, c * CW + CW)


def build_gnn(nc, a, out):
    tA = nc.dram_tensor("table_src", (N, D), F32, kind="Internal").ap()
    tB = nc.dram_tensor("table_dst", (N, D), F32, kind="Internal").ap()
    tU = nc.dram_tensor("table_logit_src", (N, M), F32, kind="Internal").ap()
    tV = nc.dram_tensor("table_logit_dst", (N, M), F32, kind="Internal").ap()
    tZ = nc.dram_tensor("table_value_dst", (N * M, D), F32, kind="Internal").ap()
    tV3 = nc.dram_tensor("table_logit_dst_parts", (N, PARTS * M), BF16, kind="Internal").ap()
    tK = nc.dram_tensor("sources_and_mod_p", (NG, 2, GE), I16, kind="Internal").ap()
    tD = nc.dram_tensor("receivers", (E,), I16, kind="Internal").ap()
    tZrow = tZ.rearrange("(n m) f -> n (m f)", m=M)
    sum0 = [nc.dram_tensor(f"sum0_{q}", (ROWS, DC), F32, kind="Internal").ap() for q in range(TG)]
    sum1 = [nc.dram_tensor(f"sum1_{q}", (ROWS, D), F32, kind="Internal").ap() for q in range(TG)]

    with ExitStack() as ctx:
        def sb(name, shape, dt=F32):
            return ctx.enter_context(nc.sbuf_tensor(name, shape, dt))

        def sem(name):
            return ctx.enter_context(nc.semaphore(name))

        pair = [ctx.enter_context(nc.psum_tensor(f"banks{k}", [128, 1024], F32)) for k in range(4)]
        bank = [pair[k // 2][:, k % 2 * 512:(k % 2 + 1) * 512] for k in range(8)]

        ident = sb("ident", [128, 128])
        tri = sb("tri", [P, P])
        trash = sb("trash", [P, 1])
        w_ab = sb("w_ab", [DC, 2 * D])
        w_ex = sb("w_ex", [128, D])
        w2 = sb("w2", [DC, D])
        w3 = sb("w3", [DC, D])
        wn1h = sb("wn1h", [DC, D])
        wn1a = sb("wn1a", [D, D])
        wn2 = sb("wn2", [DC, D])
        wn3 = sb("wn3", [DC, D])
        w_z = sb("w_z", [D, M, D])
        w_u = sb("w_u", [DC, 2 * M])
        vb = sb("vb", [P, D])
        eps_col = sb("eps_col", [P, 1])
        one_col = sb("one_col", [P, 1])
        ones = sb("ones", [1, P])
        iota_g = sb("iota_g", [P, WG])
        part = sb("part", [P, 1])

        src_i = sb("src_i", [P, NT + RB * TG], I32)
        dst_i = sb("dst_i", [P, NT + RB * TG], I32)
        src_f = sb("src_f", [P, NT])
        dst_f = sb("dst_f", [P, NT])
        wgt = sb("wgt", [P, NT])

        base_g = sb("base_g", [P, NG])
        base = sb("base", [P, NT])
        base_p = sb("base_p", [P, NG])
        rel_g = sb("rel_g", [P, NT])
        rel_t = sb("rel_t", [P, NT])
        first_of = sb("first_of", [1, NG + ZBACK, 1 + TG], I32)
        span = sb("span", [P, 8])
        flag = sb("flag", [1, 4])
        flag_i = sb("flag_i", [1, 1], I32)
        src_hi = sb("src_hi", [P, NT])
        counts = sb("counts", [P, NT])
        slot_all = sb("slot_all", [P, NT], I32)

        x = sb("x", [P, NB, D])
        h = sb("h", [P, NB, D])
        st = sb("st", [P, 6, NB])
        hT = sb("hT", [DC, N])
        sT = sb("sT", [DC, N])
        nT2 = sb("nT2", [DC, N])
        ab = sb("ab", [P, NB, 2 * D])
        sm = sb("sm", [P, TG, NB, DC])
        sq = ab[:, :, 0:D]
        raw = sm[0:IC].rearrange("p q b f -> p (q b f)")[:, 0:3 * NT // IC * P].rearrange(
            "p (k c e) -> p k c e", k=3, e=P)
        rawi = ab[0:IC].rearrange("p b f -> p (b f)")[:, 0:2 * NT // IC * P].bitcast(I32).rearrange(
            "p (k c e) -> p k c e", k=2, e=P)
        zrow = sb("zrow", [P, 2, ZC])
        vrow = sb("vrow", [P, NB, M])
        urow = sb("urow", [P, NB, M])

        X = sb("X", [128, RB, TG, 2 * D])
        Y = sb("Y", [P, 2, TG, D])
        XT = sb("XT", [128, RB, GE])
        H1 = sb("H1", [DC, RB, GE])
        H2 = sb("H2", [P, RB, TG, DC])
        KB = sb("KB", [P, RB, GE], I32)
        S = sb("S", [P, RB, TG, P])
        SL = sb("SL", [P, 2, TG, P])
        dd = sb("dd", [P, 4, TG])
        C = sb("C", [P, 2, TG, DC])
        C1 = sb("C1", [P, RB, TG, D])
        slot_s = sb("slot_s", [P, RB, TG], I32)
        slot_d = sb("slot_d", [P, 2, TG], I32)
        slot_c = sb("slot_c", [P, RB, TG], I32)
        U = sb("U", [P, RB, TG, M])
        V = sb("V", [P, 2, TG, M])
        Z = sb("Z", [P, 2, TG, ZC])
        zero = Z[:].rearrange("p j q f -> p (j q f)")[:, 0:(NB + 1) * DC].rearrange("p (b f) -> p b f", f=DC)
        KBT = sb("KBT", [WG, RB, GE], I32)
        OT = sb("OT", [WG, RB, GE])
        BW = sb("BW", [WG, RB, D])
        VW = sb("VW", [WG, RB, PARTS, M], BF16)
        L = sb("L", [P, RB, TG, M])
        EX = sb("EX", [P, RB, TG, M])
        r4 = sb("r4", [P, 4, TG])
        r8 = sb("r8", [P, TG, NB])
        abf = ab[:].rearrange("p b f -> p (b f)")
        K2 = KB[:].rearrange("p j e -> p (j e)").bitcast(I16).rearrange("p (j k e) -> p j k e", k=2, e=GE)
        KBT2 = KBT[:].rearrange("n j e -> n (j e)").bitcast(I16)[:, 0:RB * GE].rearrange("n (j e) -> n j e", j=RB)
        TM = abf[:, RB * GE // 2:RB * GE // 2 + TG * NB * M].rearrange("p (q h m) -> p q h m", q=TG, m=M)
        u_at = RB * GE // 2 + TG * NB * M
        u_parts = abf[:, u_at:u_at + PARTS * NB * M // 2].bitcast(BF16).rearrange("p (k n) -> p k n", k=PARTS)
        u_rest = abf[:, u_at + PARTS * NB * M // 2:u_at + PARTS * NB * M // 2 + NB * M]
        v_at = u_at + PARTS * NB * M // 2 + NB * M
        v_parts = abf[:, v_at:v_at + PARTS * NB * M // 2].bitcast(BF16).rearrange("p (b k m) -> p b k m", k=PARTS, m=M)
        OT1 = OT[:].rearrange("n j e -> n (j e)")[:, 0:RB * GE // 2].bitcast(BF16).rearrange("n (j e) -> n j e", j=RB)
        smf = sm[0:IC].rearrange("p q b f -> p (q b f)")
        half_w = (NT // IC * P + 1) // 2
        src16, dst16, lo16 = (smf[:, at:at + half_w].bitcast(I16)[:, 0:NT // IC * P]
                              for at in range(2 * (NT // IC * P), 2 * (NT // IC * P) + 3 * half_w, half_w))
        hi_raw = smf[:, NT // IC * P:2 * (NT // IC * P)]
        OLT = H2[:].rearrange("p j q f -> p (j q f)")[:, 0:RB * GE // 2].bitcast(BF16).rearrange(
            "p (j e) -> p j e", j=RB)
        HM = r8[:]
        flat = Z[:].rearrange("p j q f -> p (j q f)")
        at_oe, at_oh, at_end = RB * TG * WT * M, RB * TG * (WT * M + WG), RB * TG * (WT * M + WG + WT)
        Q = flat[:, 0:at_oe].rearrange("p (j q n m) -> p j q n m", j=RB, q=TG, m=M)
        OE = flat[:, at_oe:at_oh].rearrange("p (j q n) -> p j q n", j=RB, q=TG)
        OH = flat[:, at_oh:at_end].rearrange("p (j q n) -> p j q n", j=RB, q=TG)
        ZW = X[:, :, :, 0:D]
        R = XT

        weights_in = sem("weights_in")
        idx_in = sem("idx_in")
        x_in = sem("x_in")
        const_ready = sem("const_ready")
        pool_memset = sem("pool_memset")
        dve_step = sem("dve_step")
        act_step = sem("act_step")
        pe_step = sem("pe_step")
        zero_out = sem("zero_out")
        zero0_out = sem("zero0_out")
        tA_out = sem("tA_out")
        table_out = sem("table_out")
        z_out = [sem(f"z_out{k}") for k in range(2)]
        sums_in = sem("sums_in")
        y_out = sem("y_out")
        rows_in = [[sem(f"rows_in{l}_{j}") for j in range(2)] for l in range(2)]
        gat_a = [[[sem(f"gather{l}_a{j}{q}") for q in range(TG)] for j in range(RB)] for l in range(2)]
        gat_b = [[[sem(f"gather{l}_b{j}{q}") for q in range(TG)] for j in range(2)] for l in range(2)]
        scat = [[sem(f"scatter{l}_{q}") for q in range(TG)] for l in range(2)]
        retired = [sem(f"retired{l}") for l in range(2)]
        gat_v = [[sem(f"gather1_v{j}{q}") for q in range(TG)] for j in range(2)]
        pool_go = sem("pool_go")
        sp_go = sem("sp_go")
        sum_dve, sum_pe, sum_act = sem("sum_dve"), sem("sum_pe"), sem("sum_act")
        sums1_in = {half: sem(f"sums1_in_{half}") for half in ("a", "b")}
        sT_ready = sem("sT_ready")
        flag_ready = sem("flag_ready")
        win_dve = sem("win_dve")
        win_pe = sem("win_pe")
        x_load = [sem(f"x_load{j}") for j in range(RB)]
        kbt_load = [[sem(f"kbt_load{l}_{j}") for j in range(RB)] for l in range(2)]
        kb_load = [[sem(f"kb_load{l}_{j}") for j in range(RB)] for l in range(2)]
        bw_load = [sem(f"bw_load{j}") for j in range(RB)]
        zw_load = [sem(f"zw_load{j}") for j in range(RB)]
        f_T, f_XT, f_OT, f_h1, f_H1, f_h2, f_H2, f_OE, f_seg, f_acc, f_dd, f_chain, f_SL, f_cnt = (
            sem(f"f_{n}") for n in ("T", "XT", "OT", "h1", "H1", "h2", "H2", "OE", "seg", "acc", "dd", "chain", "SL", "cnt"))
        k_out = sem("k_out")
        v3_out = sem("v3_out")
        u_HM, u_log, u_max, u_sum, u_rec, u_scale, u_head, u_OH = (
            sem(f"u_{n}") for n in ("HM", "log", "max", "sum", "rec", "scale", "head", "OH"))
        u_OLT, u_cand, u_TM, u_sel = sem("u_OLT"), sem("u_cand"), sem("u_TM"), sem("u_sel")
        u_D, u_OT, u_V, u_S, u_L, u_EX, u_Q, u_R, u_RS, u_C, u_CS = (
            sem(f"u_{n}") for n in ("D", "OT", "V", "S", "L", "EX", "Q", "R", "RS", "C", "CS"))
        slots_ready = [sem(f"slots_ready{l}") for l in range(2)]
        dve_g = [sem(f"dve_group{l}") for l in range(2)]
        act_g = [sem(f"act_group{l}") for l in range(2)]
        pe_g = [sem(f"pe_group{l}") for l in range(2)]

        D0_S, D0_SL, D0_CNT, D0_ONE, D0_OFF, D0_MUL, D0_IDX, D0_SUM, D0_C, DVE0 = *range(1, 10), 9
        A0_XT, A0_H1, A0_H2, ACT0 = 1, 2, 3, 3
        P0_T, P0_H1, P0_H2, P0_C, PE0 = 1, 2, 3, 4, 4
        (D1_S, D1_SL, D1_CNT, D1_ONE, D1_OFF, D1_MUL, D1_IDX, D1_LOG, D1_MAX, D1_SUB, D1_SUM, D1_REC, D1_QS,
         D1_QW, D1_Z, D1_C, DVE1) = *range(1, 17), 16
        A1_EXP, ACT1 = 1, 1
        P1_C, PE1 = 1, 1

        OUT_HALVES = (("a", (0, NB // 2)), ("b", (NB // 2, NB)))
        FIRST = 4
        HALVES = (("'", range(FIRST)), ('"', range(FIRST, NCH)))
        Z_BLOCKS = {"'": range(2), '"': range(2, NB)}

        def blocks_in(chunks):
            return chunk_blocks(chunks[0])[0], chunk_blocks(chunks[-1])[-1] + 1

        class Steps:
            def __init__(self):
                self.n, self.at = 0, {}

            def add(self, *names):
                for name in names:
                    self.n += 1
                    self.at[name] = self.n

        dv, ac, pe_ = Steps(), Steps(), Steps()
        LN = ("mean", "xc", "sq", "var", "rstd", "norm", "relu")
        dv.add("rawf", *((n, "") for n in LN), "neg_u", "w_ex")
        for k in range(6):
            dv.add(("turned", k), ("turned_f", k))
        for half, chunks in HALVES:
            dv.add(*(("x1", c) for c in chunks), *((n, half) for n in LN))
        dv.add("vrow", "urow", "v1", "vr1", "v2", "vr2", "v3", "u1", "r1", "u2", "r2", "u3", "xb")
        dv.add(*((n, half) for half in ("a", "b") for n in ("y01", "y012", "y")))
        ac.add(("std", ""), *(("hT", c) for c in range(NCH)), *(("ab", c) for c in range(NCH)), "w3T", "w3n")
        for k in range(NCH + 1):
            ac.add(*(("g1", c) for c in (k,) if c < NCH), *(("g2", c) for c in (k - 1,) if c >= 0))
        for half, chunks in HALVES:
            ac.add(("std", half), *(("h'T", c) for c in chunks), *(("z", b) for b in Z_BLOCKS[half]))
        for k in range(6):
            pe_.add(("turn", k))
        pe_.add(*(("hT", c) for c in range(NCH)), *(("ab", c) for c in range(NCH)), "w3T", "w3n")
        for k in range(NCH + 2):
            pe_.add(*(("g1", c) for c in (k,) if c < NCH), *(("g2", c) for c in (k - 1,) if 0 <= c < NCH),
                    *(("x1", c) for c in (k - 2,) if c >= 0))
        for half, chunks in HALVES:
            pe_.add(*(("h'T", c) for c in chunks), ("u", half), *(("z", b) for b in Z_BLOCKS[half]))

        def done_dve(eng, name):
            eng.wait_ge(dve_step, dv.at[name])

        def done_act(eng, name):
            eng.wait_ge(act_step, ac.at[name])

        def done_pe(eng, name):
            eng.wait_ge(pe_step, pe_.at[name])

        DEPTH = 6

        def over_groups(eng, body):
            for s in range(2 * RB):
                body(s // RB, s % RB)
            with eng.Fori(2, TURNS) as t:
                for j in range(RB):
                    body(t, j)
            for s in range(TURNS * RB, NG + DEPTH):
                body(s // RB, s % RB)

        def back(step, t, j, k):
            jk = (j - k) % RB
            tk = t + (j - k - jk) // RB
            if not isinstance(t, int) or 0 <= RB * tk + jk < NG:
                step(tk, jk)

        def done(eng, counter, t, j, k=0):
            g = RB * t + j - k
            if not isinstance(t, int) or g >= 0:
                eng.wait_ge(counter, g + 1)

        def load_flag(eng):
            eng.wait_ge(flag_ready, 1)
            return eng.value_load(flag_i[0:1, 0:1], min_val=0, max_val=1)

        edge_in = a["edge_attr_64"]
        nodes = "(b p) f -> p b f"
        WIN_SPAN = 20
        CONSTS = 14
        K16 = 9
        WL = 19

        block = ctx.enter_context(nc.Block())

        @block.sync
        def _(sp):
            sp.dma_start(rawi[:, 0], a["src"].rearrange("(c q p) -> q c p", q=IC, p=P)).then_inc(idx_in, 16)
            sp.dma_start(rawi[:, 1], a["dst"].rearrange("(c q p) -> q c p", q=IC, p=P)).then_inc(idx_in, 16)
            sp.dma_start(raw[:, 2], a["edge_weight"].rearrange("(c q p) -> q c p", q=IC, p=P)).then_inc(idx_in, 16)
            sp.dma_start(x[:], a["x"].rearrange(nodes, p=P)).then_inc(x_in, 16)
            We1 = a["L0_gnn_We1"]
            loads = [
                (w_ex[0:D, :], We1[0:D, :]),
                (w_ab[0:D, 0:D], We1[D:2 * D, :]),
                (w_ab[0:D, D:2 * D], We1[2 * D:3 * D, :]),
                (w_ab[D:DC, 0:D], a["L0_gnn_be1"].unsqueeze(0)),
                (w2[0:D, :], a["L0_gnn_We2"]), (w2[D:DC, :], a["L0_gnn_be2"].unsqueeze(0)),
                (w3[0:D, :], a["L0_gnn_We3"]), (w3[D:DC, :], a["L0_gnn_be3"].unsqueeze(0)),
                (wn1h[0:D, :], a["L0_gnn_Wn1"][0:D, :]), (wn1h[D:DC, :], a["L0_gnn_bn1"].unsqueeze(0)),
                (wn1a[:], a["L0_gnn_Wn1"][D:2 * D, :]),
                (wn2[0:D, :], a["L0_gnn_Wn2"]), (wn2[D:DC, :], a["L0_gnn_bn2"].unsqueeze(0)),
                (wn3[0:D, :], a["L0_gnn_Wn3"]), (wn3[D:DC, :], a["L0_gnn_bn3"].unsqueeze(0)),
                (w_z[:], a["L1_gnn_var_w"].rearrange("m c d -> c m d")),
                (w_u[0:D, M:2 * M], a["L1_gnn_var_u"]), (w_u[D:DC, M:2 * M], a["L1_gnn_var_c"].unsqueeze(0)),
                (vb[:], a["L1_gnn_var_b"].partition_broadcast(P)),
            ]
            sp.wait_ge(pool_memset, 1)
            for dst, src in loads:
                sp.dma_start(dst, src).then_inc(weights_in, 16)

            for q in range(TG):
                sp.dma_start(sum1[q].rearrange(nodes, p=P), zero[:, :, 0:D]).then_inc(zero_out, 16)

            done_act(sp, ("ab", NCH - 1))
            sp.dma_start(tA.rearrange(nodes, p=P), ab[:, :, 0:D]).then_inc(tA_out, 16)
            sp.dma_start(tB.rearrange(nodes, p=P), ab[:, :, D:2 * D]).then_inc(table_out, 16)

            flag_ = load_flag(sp)
            with sp.If(flag_):
                def rows0w(t, j):
                    g = RB * t + j
                    done(sp, f_T, t, j, RB)
                    sp.dma_start(X[0:P, j, :, 0:D], edge_in[bass.ds(g * GE, GE), :].rearrange("(q p) f -> p q f", p=P)
                                 ).then_inc(x_load[j], 16)
                    done(sp, f_OT, t, j, RB)
                    sp.sem_inc(sp_go, 1)
                    sp.dma_start(KBT[:, j, :], a["dst"][bass.ds(g * GE, GE)].partition_broadcast(WG)
                                 ).then_inc(kbt_load[0][j], 16)
                    done(sp, f_h1, t, j, RB)
                    sp.sem_inc(sp_go, 1)
                    first = sp.value_load(first_of[0:1, bass.ds(g, 1), 0], min_val=0, max_val=N - WG)
                    sp.dma_start(BW[:, j, :], tB[bass.ds(first, WG), :]).then_inc(bw_load[j], 16)

                sp.wait_ge(table_out, 16)
                over_groups(sp, lambda t, j: back(rows0w, t, j, 0))

                sp.wait_ge(f_chain, K16)
                for what, k in ((src16, 0), (lo16, 1)):
                    for q in range(TG):
                        sp.dma_start(tK[:, k, q * P:(q + 1) * P].rearrange("(c g) p -> g c p", g=IC // TG),
                                     what[q::TG].rearrange("g (c p) -> g c p", p=P)).then_inc(k_out, 16)
                sp.dma_start(tD.rearrange("(c q p) -> q c p", q=IC, p=P), dst16.rearrange("q (c p) -> q c p", p=P)
                             ).then_inc(k_out, 16)
            with sp.Else():
                for q in range(TG):
                    sp.dma_start(sum0[q].rearrange(nodes, p=P), zero).then_inc(zero0_out, 16)

                def rows0(i, j):
                    g = 2 * i + j
                    sp.wait_ge(pe_g[0], g * PE0 + P0_T)
                    sp.wait_ge(dve_g[0], g * DVE0 + D0_S)
                    sp.dma_start(X[0:P, j, :, 0:D], edge_in[bass.ds(g * GE, GE), :].rearrange("(q p) f -> p q f", p=P)
                                 ).then_inc(rows_in[0][j], 16)
                    sp.dma_start(KB[:, j, :], a["dst"][bass.ds(g * GE, GE)].partition_broadcast(P)
                                 ).then_inc(rows_in[0][j], 16)

                with sp.Fori(0, PAIRS) as i:
                    rows0(i, 0)
                    rows0(i, 1)
                rows0(PAIRS, 0)

                for q in range(TG):
                    sp.wait_ge(scat[0][q], 16 * NG)
                for q in range(TG):
                    sp.dma_start(sm[:, q], sum0[q][0:N, :].rearrange(nodes, p=P)).then_inc(sums_in, 16)

            for b in range(NB):
                done_act(sp, ("z", b))
                sp.dma_start(tZrow[b * P:(b + 1) * P, :], zrow[:, b % 2, :]).then_inc(z_out[b % 2], 16)
                if b == 3:
                    done_dve(sp, "v3")
                    sp.dma_start(tV3.rearrange(nodes, p=P), v_parts.rearrange("p b k m -> p b (k m)")
                                 ).then_inc(v3_out, 16)
            sp.wait_ge(v3_out, 16)

            flag_ = load_flag(sp)
            with sp.If(flag_):
                regs = [sp.alloc_register(f"first{k}") for k in range(1 + TG)]

                def rows1w(t, j, first):
                    done(sp, u_V, t, j, RB)
                    sp.sem_inc(sp_go, 1)
                    sp.dma_start(VW[:, j].rearrange("n k m -> n (k m)"), tV3[bass.ds(first, WG), :]
                                 ).then_inc(bw_load[j], 16)

                def rows1z(t, j, firsts):
                    done(sp, u_C, t, j, RB)
                    if isinstance(t, int) and t == j == 0:
                        for k in range(2):
                            sp.wait_ge(z_out[k], 16 * len(range(k, NB, 2)))
                    sp.sem_inc(sp_go, 1)
                    for q in range(TG):
                        sp.dma_start(ZW[:, j, q, :], tZ[bass.ds(firsts[q] * M, WT * M), :]).then_inc(zw_load[j], 16)

                def body1w(t, j):
                    if isinstance(t, int) and RB * t + j >= NG + ZBACK:
                        return
                    sp.load(regs, first_of[0:1, bass.ds(RB * t + j, 1), :])
                    firsts = ([sp.snap(regs[0], min_val=0, max_val=N - WG)]
                              + [sp.snap(r, min_val=0, max_val=N - WT) for r in regs[1:]])
                    back(lambda t, j: rows1w(t, j, firsts[0]), t, j, 0)
                    back(lambda t, j: rows1z(t, j, firsts[1:]), t, j, ZBACK)

                over_groups(sp, body1w)
            with sp.Else():
                done_dve(sp, "urow")
                sp.dma_start(tU.rearrange(nodes, p=P), urow[:]).then_inc(table_out, 16)
                sp.dma_start(tV.rearrange(nodes, p=P), vrow[:]).then_inc(table_out, 16)

                def rows1(i, j):
                    g = 2 * i + j
                    sp.wait_ge(dve_g[1], g * DVE1 + D1_S)
                    sp.dma_start(KB[:, j, :], a["src"][bass.ds(g * GE, GE)].partition_broadcast(P)
                                 ).then_inc(rows_in[1][j], 16)

                with sp.Fori(0, PAIRS) as i:
                    rows1(i, 0)
                    rows1(i, 1)
                rows1(PAIRS, 0)

            for q in range(TG):
                sp.wait_ge(scat[1][q], 16 * NG)
            for half, (b0, b1) in OUT_HALVES:
                for q in range(TG):
                    sp.dma_start(sm[:, q, b0:b1, 0:D], sum1[q][b0 * P:b1 * P, :].rearrange(nodes, p=P)
                                 ).then_inc(sums1_in[half], 16)
            for half, (b0, b1) in OUT_HALVES:
                done_dve(sp, ("y", half))
                sp.dma_start(out[b0 * P:b1 * P, :].rearrange(nodes, p=P), h[:, b0:b1, :]).then_inc(y_out, 16)
            sp.wait_ge(y_out, 32)

        @block.gpsimd
        def _(pool):
            pool.memset(w_ab[:], 0.0)
            pool.memset(w_u[:], 0.0)
            pool.memset(zero, 0.0).then_inc(pool_memset, 1)
            pool.memset(ident[:], 0.0).then_inc(const_ready, 1)
            pool.wait_ge(const_ready, 1)
            pool.affine_select(out=ident[:], in_=ident[:], compare_op=ALU.not_equal, fill=1.0, base=0,
                               pattern=[[-1, 128]], channel_multiplier=1).then_inc(const_ready, 1)
            pool.wait_ge(const_ready, 2)
            pool.memset(tri[:], 1.0).then_inc(const_ready, 1)
            pool.wait_ge(const_ready, 3)
            pool.affine_select(out=tri[:], in_=tri[:], compare_op=ALU.is_gt, fill=0.0, base=0,
                               pattern=[[-1, P]], channel_multiplier=1).then_inc(const_ready, 1)
            pool.iota(trash[:], [[0, 1]], base=TRASH, channel_multiplier=1,
                      allow_small_or_imprecise_dtypes=True).then_inc(const_ready, 1)

            pool.iota(part[:], [[0, 1]], base=0, channel_multiplier=1,
                      allow_small_or_imprecise_dtypes=True).then_inc(const_ready, 1)
            pool.iota(iota_g[:], [[1, WG]], base=0, channel_multiplier=0,
                      allow_small_or_imprecise_dtypes=True).then_inc(const_ready, 1)

            for n, (what, value) in enumerate((
                    (hT[D:DC, :], 1.0), (H1[D:DC, :, :], 1.0), (H2[:, :, :, D:DC], 1.0),
                    (src_i[:, NT:], 0), (dst_i[:, NT:], 0), (sT[:], 0.0), (nT2[D:DC, :], 1.0))):
                pool.wait_ge(const_ready, CONSTS - 7 + n)
                pool.memset(what, value).then_inc(const_ready, 1)

            def gathers0w(t, j):
                done(pool, slots_ready[0], t, j)
                pool.sem_inc(pool_go, 1)
                for q in range(TG):
                    pool.indirect_dma_start(X[0:P, j, q, D:2 * D], None, tA,
                                            bass.IndirectOffsetOnAxis(ap=slot_s[:, j, q:q + 1], axis=0)
                                            ).then_inc(gat_a[0][j][q], 16)

            def scatters1w(t, j):
                done(pool, u_CS, t, j)
                for q in range(TG):
                    pool.wait_ge(scat[1][q], 16 * (RB * t + j))
                    pool.sem_inc(retired[1], 1)
                    pool.indirect_dma_start(sum1[q], bass.IndirectOffsetOnAxis(ap=slot_c[:, j, q:q + 1], axis=0),
                                            C1[:, j, q, :], None, compute_op=ALU.add).then_inc(scat[1][q], 16)

            def body1w(t, j):
                back(scatters1w, t, j, 5)

            def gathers(l, i, j):
                g = 2 * i + j
                pool.wait_ge(slots_ready[l], g + 1)
                pool.sem_inc(pool_go, 1)
                for q in range(TG):
                    to_a = X[0:P, j, q, D:2 * D] if l == 0 else U[:, j, q, :]
                    to_b = Y[:, j, q, :] if l == 0 else Z[:, j, q, :]
                    pool.indirect_dma_start(to_a, None, tA if l == 0 else tU,
                                            bass.IndirectOffsetOnAxis(ap=slot_s[:, j, q:q + 1], axis=0)
                                            ).then_inc(gat_a[l][j][q], 16)
                    pool.indirect_dma_start(to_b, None, tB if l == 0 else tZrow,
                                            bass.IndirectOffsetOnAxis(ap=slot_d[:, j, q:q + 1], axis=0)
                                            ).then_inc(gat_b[l][j][q], 16)
                    if l == 1:
                        pool.indirect_dma_start(V[:, j, q, :], None, tV,
                                                bass.IndirectOffsetOnAxis(ap=slot_d[:, j, q:q + 1], axis=0)
                                                ).then_inc(gat_v[j][q], 16)

            def scatters(l, i, j):
                g = 2 * i + j
                for q in range(TG):
                    pool.wait_ge(scat[l][q], 16 * g)
                    pool.sem_inc(retired[l], 1)
                pool.wait_ge(dve_g[l], g * (DVE0, DVE1)[l] + (D0_C, D1_C)[l] + 2 * (DVE0, DVE1)[l])
                pool.sem_inc(pool_go, 1)
                for q in range(TG):
                    pool.indirect_dma_start((sum0, sum1)[l][q],
                                            bass.IndirectOffsetOnAxis(ap=slot_c[:, j, q:q + 1], axis=0),
                                            (C, C1)[l][:, j, q, :], None, compute_op=ALU.add
                                            ).then_inc(scat[l][q], 16)

            for l in range(2):
                if l == 0:
                    pool.wait_ge(tA_out, 16)
                else:
                    pool.wait_ge(zero_out, 16 * TG)
                flag_ = load_flag(pool)
                with pool.If(flag_):
                    if l == 0:
                        over_groups(pool, lambda t, j: back(gathers0w, t, j, 0))
                    else:
                        over_groups(pool, body1w)
                with pool.Else():
                    if l == 0:
                        pool.wait_ge(table_out, 16)
                        pool.wait_ge(zero0_out, 16 * TG)
                    else:
                        pool.wait_ge(table_out, 48)
                        for k in range(2):
                            pool.wait_ge(z_out[k], 16 * len(range(k, NB, 2)))
                    gathers(l, 0, 0)
                    with pool.Fori(0, PAIRS) as i:
                        gathers(l, i, 1)
                        scatters(l, i, 0)
                        gathers(l, i + 1, 0)
                        scatters(l, i, 1)
                    scatters(l, PAIRS, 0)

        @block.scalar
        def _(act):
            def norm_std(t, b0, b1):
                done_dve(act, ("var", t))
                act.activation(st[:, 2, b0:b1], st[:, 1, b0:b1], ACT.Sqrt, bias=eps_col[:, 0:1], scale=1.0 / D
                               ).then_inc(act_step, 1)

            def slots(l, i, j):
                g = 2 * i + j
                act.copy(slot_s[:, j, :], src_i[:, bass.ds(g * TG, TG)])
                act.copy(slot_d[:, j, :], dst_i[:, bass.ds(g * TG, TG)]).then_inc(slots_ready[l], 1)

            norm_std("", 0, NB)
            for c in range(NCH):
                lo, hi = chunk_cols(c)
                done_pe(act, ("hT", c))
                act.copy(hT[0:D, lo:hi], bank[c % 2][0:D, 0:hi - lo]).then_inc(act_step, 1)

            for c in range(NCH):
                b = chunk_blocks(c)
                done_pe(act, ("ab", c))
                act.copy(ab[:, b[0]:b[-1] + 1, :], bank[c % 2][0:P, 0:len(b) * 2 * D].rearrange(
                    "p (b f) -> p b f", f=2 * D)).then_inc(act_step, 1)

            done_pe(act, "w3T")
            act.copy(XT[0:D, 0, 0:DC], bank[5][0:D, 0:DC]).then_inc(act_step, 1)
            done_pe(act, "w3n")
            act.copy(w3[:], bank[6][0:DC, 0:D]).then_inc(act_step, 1)

            def group0(i, j):
                g = 2 * i + j
                act.wait_ge(pe_g[0], (g + 2) * PE0 + P0_T)
                act.copy(XT[:, j, :], bank[j % 2][:, 0:GE]).then_inc(act_g[0], 1)
                slots(0, i + 1, j)
                act.wait_ge(pe_g[0], (g + 2) * PE0 + P0_H1)
                act.activation(H1[0:D, j, :], bank[2 + j % 2][0:D, 0:GE], ACT.Relu).then_inc(act_g[0], 1)
                act.wait_ge(pe_g[0], (g + 2) * PE0 + P0_H2)
                act.activation(H2[:, j, :, 0:D], bank[4 + j % 2][0:P, 0:TG * D].rearrange("p (q f) -> p q f", q=TG),
                               ACT.Relu).then_inc(act_g[0], 1)

            act.wait_ge(const_ready, CONSTS)
            done_dve(act, ("turned_f", 5))
            act.sem_inc(act_g[0], 2 * ACT0)
            act.sem_inc(act_g[1], 2 * ACT1)

            def slots_w(l, t, j):
                act.copy(slot_s[:, j, :], src_i[:, bass.ds((RB * t + j) * TG, TG)]).then_inc(slots_ready[l], 1)

            def turned_w(t, j):
                done(act, f_T, t, j)
                done(act, f_h1, t, j, RB)
                act.copy(XT[:, j, :], bank[j % 2][:, 0:GE]).then_inc(f_XT, 1)
                slots_w(0, t + 1, j)

            def hidden1_w(t, j):
                done(act, f_h1, t, j)
                done(act, f_h2, t, j, RB)
                act.activation(H1[0:D, j, :], bank[2 + j % 2][0:D, 0:GE], ACT.Relu).then_inc(f_H1, 1)

            def hidden2_w(t, j):
                done(act, f_h2, t, j)
                done(act, f_seg, t, j, RB)
                act.activation(H2[:, j, :, 0:D], bank[4 + j % 2][0:P, 0:TG * D].rearrange("p (q f) -> p q f", q=TG),
                               ACT.Relu).then_inc(f_H2, 1)

            def sources0_w(t, j):
                done(act, f_SL, t, j, RB)
                act.dma_start(KB[:, j, :], a["src"][bass.ds((RB * t + j) * GE, GE)].partition_broadcast(P)
                              ).then_inc(kb_load[0][j], 16)

            def body0w(t, j):
                back(sources0_w, t, j, -2)
                back(turned_w, t, j, 0)
                back(hidden1_w, t, j, 1)
                back(hidden2_w, t, j, 2)

            flag_ = load_flag(act)
            with act.If(flag_):
                for j in range(RB):
                    slots_w(0, 0, j)
                sources0_w(0, 0)
                sources0_w(0, 1)
                over_groups(act, body0w)
            with act.Else():
                slots(0, 0, 0)
                slots(0, 0, 1)
                with act.Fori(0, PAIRS) as i:
                    group0(i, 0)
                    group0(i, 1)
                group0(PAIRS, 0)
                for c in range(NCH):
                    lo, hi = chunk_cols(c)
                    act.wait_ge(sum_pe, c + 1)
                    act.copy(sT[:, lo:hi], bank[c % 2][0:DC, 0:hi - lo]).then_inc(sum_act, 1)
                act.wait_ge(sum_act, NCH)
                act.sem_inc(sT_ready, 1)

            def hidden(s, to, from_, c):
                lo, hi = chunk_cols(c)
                done_pe(act, (s, c))
                act.activation(to[0:D, lo:hi], bank[from_ + c % 2][0:D, 0:hi - lo], ACT.Relu).then_inc(act_step, 1)

            for k in range(NCH + 1):
                if k < NCH:
                    hidden("g1", hT, 0, k)
                if k >= 1:
                    hidden("g2", nT2, 2, k - 1)

            def rows1_w(t, j):
                at = bass.ds((RB * t + j) * GE, GE)
                done(act, u_OT, t, j, RB)
                act.dma_start(KBT2[:, j, :], tD[at].partition_broadcast(WG)).then_inc(kbt_load[1][j], 16)
                done(act, u_OLT, t, j, RB)
                act.dma_start(K2[:, j].rearrange("p k e -> p (k e)"),
                              tK[bass.ds(RB * t + j, 1)].rearrange("g k e -> (g k e)").partition_broadcast(P)
                              ).then_inc(kb_load[1][j], 16)

            for half, chunks in HALVES:
                norm_std(half, *blocks_in(chunks))
                for c in chunks:
                    lo, hi = chunk_cols(c)
                    done_pe(act, ("h'T", c))
                    act.copy(hT[0:D, lo:hi], bank[c % 2][0:D, 0:hi - lo]).then_inc(act_step, 1)
                if half == '"':
                    with act.If(load_flag(act)):
                        act.wait_ge(f_dd, 1)
                        act.wait_ge(k_out, 16 * (2 * TG + 1))
                        rows1_w(0, 0)
                        rows1_w(0, 1)
                for b in Z_BLOCKS[half]:
                    done_pe(act, ("z", b))
                    if b >= 2:
                        act.wait_ge(z_out[b % 2], 16 * (b // 2))
                    act.copy(zrow[:, b % 2, 0:M * D], bank[2 + b % 2][0:P, :]).then_inc(act_step, 1)

            def group1(i, j):
                g = 2 * i + j
                act.wait_ge(dve_g[1], (g + 2) * DVE1 + D1_SUB)
                act.activation(EX[:, j], L[:, j], ACT.Exp).then_inc(act_g[1], 1)
                act.wait_ge(pe_g[1], (g + 2) * PE1 + P1_C)
                slots(1, i + 1, j)

            def exps_w(t, j):
                done(act, u_L, t, j)
                act.activation(EX[:, j], L[:, j], ACT.Exp).then_inc(u_EX, 1)

            def reduced_w(t, j):
                done(act, u_R, t, j)
                act.copy(R[:, j, :], bank[2 + j % 2][:, 0:GE]).then_inc(u_RS, 1)

            def combined_w(t, j):
                g = RB * t + j
                done(act, u_C, t, j)
                act.wait_ge(retired[1], TG * g)
                act.copy(slot_c[:, j, :], slot_all[:, bass.ds(g * TG, TG)])
                act.copy(C1[:, j], bank[5][0:P, 0:TG * D].rearrange("p (q f) -> p q f", q=TG)).then_inc(u_CS, 1)

            def differences(t, j):
                act.wait_ge(kb_load[1][j], (t + 1) * 16)
                for q in range(TG):
                    last = act.activation(S[:, j, q, :], K2[:, j, 0, q * P:(q + 1) * P], ACT.Abs,
                                          bias=src_f[:, bass.ds((RB * t + j) * TG + q, 1)], scale=-1.0)
                last.then_inc(u_D, 1)

            def same_source(t, j):
                done(act, u_D, t, j)
                act.activation(S[:, j], S[:, j], ACT.Relu, bias=one_col[:, 0:1], scale=-1.0).then_inc(u_S, 1)

            def body1w(t, j):
                back(rows1_w, t, j, -2)
                back(differences, t, j, 1)
                back(exps_w, t, j, 2)
                back(reduced_w, t, j, 4)
                back(same_source, t, j, 1)
                back(combined_w, t, j, 5)

            flag_ = load_flag(act)
            with act.If(flag_):
                over_groups(act, body1w)
            with act.Else():
                slots(1, 0, 0)
                slots(1, 0, 1)
                with act.Fori(0, PAIRS) as i:
                    group1(i, 0)
                    group1(i, 1)
                group1(PAIRS, 0)

        @block.vector
        def _(dve):
            def step(ins):
                ins.then_inc(dve_step, 1)

            windows = [0]

            def win(ins):
                windows[0] += 1
                ins.then_inc(win_dve, 1)
                dve.wait_ge(win_dve, windows[0])

            def layer_norm(t, b0, b1):
                xs, hs, sqs = x[:, b0:b1, :], h[:, b0:b1, :], sq[:, b0:b1, :]
                step(dve.tensor_reduce(st[:, 0, b0:b1], xs, AX_X, ALU.add))
                done_dve(dve, ("mean", t))
                step(dve.scalar_tensor_tensor(out=hs, in0=st[:, 0, b0:b1].unsqueeze(2).to_broadcast([P, b1 - b0, D]),
                                              scalar=-1.0 / D, in1=xs, op0=ALU.mult, op1=ALU.add))
                done_dve(dve, ("xc", t))
                step(dve.tensor_tensor(sqs, hs, hs, ALU.mult))
                done_dve(dve, ("sq", t))
                step(dve.tensor_reduce(st[:, 1, b0:b1], sqs, AX_X, ALU.add))
                done_act(dve, ("std", t))
                step(dve.reciprocal(st[:, 3, b0:b1], st[:, 2, b0:b1]))
                done_dve(dve, ("rstd", t))
                step(dve.tensor_tensor(hs, hs, st[:, 3, b0:b1].unsqueeze(2).to_broadcast([P, b1 - b0, D]), ALU.mult))
                done_dve(dve, ("norm", t))
                step(dve.tensor_scalar(hs, hs, 0.0, None, ALU.max))

            dve.memset(eps_col[:], EPS)
            dve.memset(one_col[:], 1.0)
            win(dve.memset(ones[:], 1.0))
            dve.wait_ge(idx_in, 48)
            step(dve.tensor_copy(raw[:, 0:2], rawi))

            done_dve(dve, "rawf")
            dve.wait_ge(x_in, 16)
            layer_norm("", 0, NB)

            def chain(ins, n):
                ins.then_inc(f_chain, 1)
                dve.wait_ge(f_chain, n)

            def blocks_of(to, from_, n):
                chain(dve.tensor_scalar(to, from_, 1.0 / P, -(P - 1) / 2.0 / P, ALU.mult, ALU.add), n)
                chain(dve.tensor_scalar(to, to, ROUND, None, ALU.add), n + 1)
                chain(dve.tensor_scalar(to, to, -ROUND, None, ALU.add), n + 2)

            dve.wait_ge(weights_in, 16 * WL)
            step(dve.tensor_scalar(w_u[0:D, 0:M], w_u[0:D, M:2 * M], -1.0, None, ALU.mult))
            dve.wait_ge(const_ready, 2)
            step(dve.tensor_copy(w_ex[D:2 * D, :], ident[D:2 * D, D:2 * D]))
            for k in range(6):
                what, half = k // 2, k % 2
                lo, hi = (0, 6 * IC) if half == 0 else (6 * IC, NT)
                done_pe(dve, ("turn", k))
                t = (src_i, dst_i, wgt)[what]
                tf = (src_f, dst_f, wgt)[what]
                step(dve.tensor_copy(t[:, lo:hi], bank[2 + k][0:P, 0:hi - lo]))
                if what == 2:
                    done_dve(dve, ("turned", k))
                step(dve.tensor_copy(tf[:, lo:hi], bank[2 + k][0:P, 0:hi - lo]))
            for k in range(2):
                lo, hi = (0, 6 * IC) if k == 0 else (6 * IC, NT)
                dve.wait_ge(win_pe, k + 1)
                win(dve.tensor_copy(base[:, lo:hi], bank[2 + k][0:P, 0:hi - lo]))
            win(dve.tensor_scalar(base_g[:], base[:, 0:NT:TG], float(N - WG), None, ALU.min))
            win(dve.tensor_scalar(base[:], base[:], float(N - WT), None, ALU.min))
            win(dve.memset(first_of[:], 0))
            win(dve.tensor_copy(first_of[:, 0:NG, 0], base_g[0:1, :]))
            win(dve.tensor_copy(first_of[:, ZBACK:, 1:], base[0:1, :].rearrange("p (g q) -> p g q", q=TG)))
            dve.wait_ge(const_ready, 6)
            win(dve.tensor_scalar(base_p[:], base_g[:], part[:, 0:1], None, ALU.add))
            win(dve.tensor_tensor(rel_g[:].rearrange("p (g q) -> p g q", q=TG),
                                  dst_f[:].rearrange("p (g q) -> p g q", q=TG),
                                  base_g[:].unsqueeze(2).to_broadcast([P, NG, TG]), ALU.subtract))
            win(dve.tensor_tensor(rel_t[:], dst_f[:], base[:], ALU.subtract))
            win(dve.tensor_reduce(span[:, 0:1], rel_g[:], AX_X, ALU.max))
            win(dve.tensor_reduce(span[:, 1:2], rel_g[:], AX_X, ALU.min))
            win(dve.tensor_reduce(span[:, 2:3], rel_t[:], AX_X, ALU.max))
            win(dve.tensor_reduce(span[:, 3:4], rel_t[:], AX_X, ALU.min))
            win(dve.tensor_scalar(span[:, 4:5], span[:, 0:1], float(1 - WG), None, ALU.add))
            win(dve.tensor_scalar(span[:, 5:6], span[:, 2:3], float(1 - WT), None, ALU.add))
            win(dve.tensor_scalar(span[:, 6:7], span[:, 1:2], -1.0, None, ALU.mult))
            win(dve.tensor_scalar(span[:, 7:8], span[:, 3:4], -1.0, None, ALU.mult))
            win(dve.tensor_reduce(span[:, 0:1], span[:, 4:8], AX_X, ALU.max))
            dve.wait_ge(win_pe, 3)
            win(dve.tensor_reduce(flag[:, 0:1], bank[4][0:1, 0:P], AX_X, ALU.max))
            win(dve.tensor_scalar(flag[:, 1:2], flag[:, 0:1], 0.0, None, ALU.is_le))
            dve.tensor_copy(flag_i[:], flag[:, 1:2]).then_inc(flag_ready, 1)

            dve.sem_inc(dve_g[0], 2 * DVE0)
            dve.sem_inc(dve_g[1], 2 * DVE1)
            dve.wait_ge(const_ready, CONSTS)

            def equal_rows(l, i, j, keys):
                g = 2 * i + j
                base, s = (g + 2) * (DVE0, DVE1)[l], dve_g[l]
                kf = keys[:, bass.ds(g * TG, TG)]
                dve.wait_ge(rows_in[l][j], (i + 1) * (32, 16)[l])
                dve.wait_ge(pe_g[l], (g + 1) * (PE0, PE1)[l])
                dve.tensor_tensor(S[:, j], KB[:, j, :].rearrange("p (q f) -> p q f", q=TG),
                                  kf.unsqueeze(2).to_broadcast([P, TG, P]), ALU.is_equal).then_inc(s, 1)
                dve.wait_ge(s, base + D0_S)
                dve.tensor_tensor(SL[:, 0], S[:, j], tri[:].unsqueeze(1).to_broadcast([P, TG, P]),
                                  ALU.mult).then_inc(s, 1)
                dve.wait_ge(s, base + D0_SL)
                dve.tensor_reduce(dd[:, 0], SL[:, 0], AX_X, ALU.add).then_inc(s, 1)
                dve.wait_ge(s, base + D0_CNT)
                dve.tensor_scalar(dd[:, 1], dd[:, 0], 1.0, None, ALU.min).then_inc(s, 1)
                dve.tensor_scalar(dd[:, 2], kf, -1.0, trash[:, 0:1], ALU.mult, ALU.add).then_inc(s, 1)
                dve.wait_ge(s, base + D0_OFF)
                dve.tensor_tensor(dd[:, 3], dd[:, 1], dd[:, 2], ALU.mult).then_inc(s, 1)
                dve.wait_ge(s, base + D0_MUL)
                dve.wait_ge(retired[l], TG * g)
                dve.tensor_tensor(slot_c[:, j, :], dd[:, 3], kf, ALU.add).then_inc(s, 1)

            def group0(i, j):
                g = 2 * i + j
                base = (g + 2) * DVE0
                equal_rows(0, i, j, dst_f)
                for q in range(TG):
                    dve.wait_ge(gat_a[0][j][q], (i + 1) * 16)
                    dve.wait_ge(gat_b[0][j][q], (i + 1) * 16)
                dve.tensor_tensor(X[0:P, j, :, D:2 * D], X[0:P, j, :, D:2 * D], Y[:, j], ALU.add).then_inc(dve_g[0], 1)
                dve.wait_ge(pe_g[0], (g + 2) * PE0 + P0_C)
                dve.tensor_copy(C[:, j], bank[6 + j % 2][0:P, 0:TG * DC].rearrange("p (q f) -> p q f", q=TG)
                                ).then_inc(dve_g[0], 1)

            def window_t(t, j):
                dve.wait_ge(kbt_load[0][j], (t + 1) * 16)
                done(dve, f_h1, t, j, RB)
                dve.tensor_scalar(OT[:, j, :], KBT[:, j, :], base_p[0:WG, bass.ds(RB * t + j, 1)], None,
                                  ALU.is_equal).then_inc(f_OT, 1)

            def window_e(t, j):
                done(dve, f_seg, t, j, RB)
                dve.tensor_tensor(OE[:, j], iota_g[:].unsqueeze(1).to_broadcast([P, TG, WG]),
                                  rel_g[:, bass.ds((RB * t + j) * TG, TG)].unsqueeze(2).to_broadcast([P, TG, WG]),
                                  ALU.is_equal).then_inc(f_OE, 1)

            def add_window(t, j):
                done(dve, f_seg, t, j)
                done(dve, f_acc, t, j, 1)
                first = dve.value_load(first_of[0:1, bass.ds(RB * t + j, 1), 0], min_val=0, max_val=N - WG)
                to = sT[:, bass.ds(first, WG)]
                dve.tensor_tensor(to, to, bank[6 + j % 2][0:DC, 0:WG], ALU.add).then_inc(f_acc, 1)

            def same_before(t, j):
                g = RB * t + j
                dve.wait_ge(kb_load[0][j], (t + 1) * 16)
                done(dve, f_cnt, t, j, 2)
                for q in range(TG):
                    last = dve.scalar_tensor_tensor(out=SL[:, j % 2, q, :], in0=KB[:, j, q * P:(q + 1) * P],
                                                    scalar=src_f[:, bass.ds(g * TG + q, 1)], in1=tri[:],
                                                    op0=ALU.is_equal, op1=ALU.mult)
                last.then_inc(f_SL, 1)

            def count_before(t, j):
                g = RB * t + j
                done(dve, f_SL, t, j)
                dve.tensor_reduce(counts[:, bass.ds(g * TG, TG)], SL[:, j % 2], AX_X, ALU.add).then_inc(f_cnt, 1)

            def body0w(t, j):
                back(window_t, t, j, 0)
                back(same_before, t, j, 1)
                back(window_e, t, j, 2)
                back(count_before, t, j, 1)
                back(add_window, t, j, 3)

            flag_ = load_flag(dve)
            with dve.If(flag_):
                over_groups(dve, body0w)
                dve.wait_ge(f_acc, NG)
                dve.sem_inc(sT_ready, 1)
                dve.wait_ge(f_cnt, NG)
                chain(dve.tensor_scalar(counts[:], counts[:], 1.0, None, ALU.min), 1)
                chain(dve.tensor_scalar(base[:], src_f[:], -1.0, trash[:, 0:1], ALU.mult, ALU.add), 2)
                chain(dve.tensor_tensor(base[:], base[:], counts[:], ALU.mult), 3)
                dve.tensor_tensor(slot_all[:], base[:], src_f[:], ALU.add).then_inc(f_dd, 1)
                src_raw = raw[:, 0].rearrange("p c e -> p (c e)")
                chain(dve.tensor_copy(dst16, raw[:, 1].rearrange("p c e -> p (c e)")), 4)
                chain(dve.tensor_copy(src16, src_raw), 5)
                blocks_of(hi_raw, src_raw, 6)
                chain(dve.scalar_tensor_tensor(out=lo16, in0=hi_raw, scalar=-float(P), in1=src_raw,
                                               op0=ALU.mult, op1=ALU.add), K16)
                blocks_of(src_hi[:], src_f[:], K16 + 1)
            with dve.Else():
                with dve.Fori(0, PAIRS) as i:
                    group0(i, 0)
                    group0(i, 1)
                group0(PAIRS, 0)
                dve.wait_ge(sums_in, 16 * TG)
                dve.tensor_tensor(sm[:, 0], sm[:, 0], sm[:, 1], ALU.add).then_inc(sum_dve, 1)
                dve.wait_ge(sum_dve, 1)
                dve.tensor_tensor(sm[:, 0], sm[:, 0], sm[:, 2], ALU.add).then_inc(sum_dve, 1)

            for half, chunks in HALVES:
                for c in chunks:
                    b = chunk_blocks(c)
                    done_pe(dve, ("x1", c))
                    step(dve.tensor_tensor(x[:, b[0]:b[-1] + 1, :], x[:, b[0]:b[-1] + 1, :], bank[4 + c % 2][
                        0:P, 0:len(b) * D].rearrange("p (b f) -> p b f", f=D), ALU.add))
                done_dve(dve, ("x1", chunks[-1]))
                layer_norm(half, *blocks_in(chunks))
            done_pe(dve, ("u", '"'))
            logits_of = bank[6][0:P, 0:NB * 2 * M].rearrange("p (b m) -> p b m", m=2 * M)
            step(dve.tensor_copy(vrow[:], logits_of[:, :, 0:M]))
            step(dve.tensor_copy(urow[:], logits_of[:, :, M:2 * M]))

            def group1(i, j):
                g = 2 * i + j
                base, s = (g + 2) * DVE1, dve_g[1]
                equal_rows(1, i, j, src_f)
                for q in range(TG):
                    dve.wait_ge(gat_a[1][j][q], (i + 1) * 16)
                    dve.wait_ge(gat_b[1][j][q], (i + 1) * 16)
                    dve.wait_ge(gat_v[j][q], (i + 1) * 16)
                dve.tensor_tensor(L[:, j], U[:, j], V[:, j], ALU.add).then_inc(s, 1)
                dve.wait_ge(s, base + D1_LOG)
                dve.tensor_reduce(r4[:, 0], L[:, j], AX_X, ALU.max).then_inc(s, 1)
                dve.wait_ge(s, base + D1_MAX)
                dve.tensor_tensor(L[:, j], L[:, j], r4[:, 0].unsqueeze(2).to_broadcast([P, TG, M]),
                                  ALU.subtract).then_inc(s, 1)
                dve.wait_ge(act_g[1], (g + 2) * ACT1 + A1_EXP)
                dve.tensor_reduce(r4[:, 1], EX[:, j], AX_X, ALU.add).then_inc(s, 1)
                dve.wait_ge(s, base + D1_SUM)
                dve.reciprocal(r4[:, 2], r4[:, 1]).then_inc(s, 1)
                dve.wait_ge(s, base + D1_REC)
                dve.tensor_tensor(r4[:, 3], r4[:, 2], wgt[:, bass.ds(g * TG, TG)], ALU.mult).then_inc(s, 1)
                dve.wait_ge(s, base + D1_QS)
                dve.tensor_tensor(EX[:, j], EX[:, j], r4[:, 3].unsqueeze(2).to_broadcast([P, TG, M]),
                                  ALU.mult).then_inc(s, 1)
                dve.wait_ge(s, base + D1_QW)
                for q in range(TG):
                    zq = Z[:, j, q, 0:M * D].rearrange("p (m f) -> p m f", m=M)
                    last = dve.tensor_tensor(zq, zq, EX[:, j, q].unsqueeze(2).to_broadcast([P, M, D]), ALU.mult)
                last.then_inc(s, 1)
                dve.wait_ge(pe_g[1], (g + 2) * PE1 + P1_C)
                dve.tensor_copy(C1[:, j], bank[6 + j % 2][0:P, 0:TG * D].rearrange("p (q f) -> p q f", q=TG)
                                ).then_inc(s, 1)

            rest = u_rest.rearrange("p (b m) -> p b m", m=M)
            done_dve(dve, "urow")
            step(dve.tensor_copy(v_parts[:, :, 0, :], vrow[:]))
            done_dve(dve, "v1")
            step(dve.tensor_tensor(rest, vrow[:], v_parts[:, :, 0, :], ALU.subtract))
            done_dve(dve, "vr1")
            step(dve.tensor_copy(v_parts[:, :, 1, :], rest))
            done_dve(dve, "v2")
            step(dve.tensor_tensor(rest, rest, v_parts[:, :, 1, :], ALU.subtract))
            done_dve(dve, "vr2")
            step(dve.tensor_copy(v_parts[:, :, 2, :], rest))
            done_dve(dve, "v3")
            of_u = urow[:].rearrange("p b m -> p (b m)")
            step(dve.tensor_copy(u_parts[:, 0, :], of_u))
            done_dve(dve, "u1")
            step(dve.tensor_tensor(u_rest, of_u, u_parts[:, 0, :], ALU.subtract))
            done_dve(dve, "r1")
            step(dve.tensor_copy(u_parts[:, 1, :], u_rest))
            done_dve(dve, "u2")
            step(dve.tensor_tensor(u_rest, u_rest, u_parts[:, 1, :], ALU.subtract))
            done_dve(dve, "r2")
            step(dve.tensor_copy(u_parts[:, 2, :], u_rest))
            step(dve.tensor_tensor(x[:], x[:], vb[:].unsqueeze(1).to_broadcast([P, NB, D]), ALU.add))

            def window1_t(t, j):
                dve.wait_ge(kbt_load[1][j], (t + 1) * 16)
                dve.tensor_scalar(OT1[:, j, :], KBT2[:, j, :], base_p[0:WG, bass.ds(RB * t + j, 1)], None,
                                  ALU.is_equal).then_inc(u_OT, 1)

            def sources_t(t, j):
                dve.wait_ge(kb_load[1][j], (t + 1) * 16)
                dve.tensor_scalar(OLT[:, j, :], K2[:, j, 1, :], part[:, 0:1], None, ALU.is_equal).then_inc(u_OLT, 1)

            def block_mask(t, j):
                dve.tensor_tensor(HM, iota_g[:, 0:NB].unsqueeze(1).to_broadcast([P, TG, NB]),
                                  src_hi[:, bass.ds((RB * t + j) * TG, TG)].unsqueeze(2).to_broadcast([P, TG, NB]),
                                  ALU.is_equal).then_inc(u_HM, 1)

            def choose(t, j):
                done(dve, u_HM, t, j)
                done(dve, u_cand, t, j)
                cand = pair[3 * (j % 2)][0:P, 0:TG * TW].rearrange("p (q n) -> p q n", q=TG)[:, :, 0:NB * M]
                dve.tensor_tensor(TM, cand.rearrange("p q (h m) -> p q h m", m=M),
                                  HM.unsqueeze(3).to_broadcast([P, TG, NB, M]), ALU.mult).then_inc(u_TM, 1)

            def source_logits(t, j):
                done(dve, u_TM, t, j)
                dve.tensor_reduce(U[:, j], TM.rearrange("p q h m -> p q m h"), AX_X, ALU.add).then_inc(u_sel, 1)

            def logits(t, j):
                done(dve, u_sel, t, j)
                done(dve, u_V, t, j)
                dve.tensor_tensor(L[:, j], U[:, j], bank[4][0:P, 0:TG * M].rearrange(
                    "p (q m) -> p q m", q=TG), ALU.add).then_inc(u_log, 1)

            def logits_max(t, j):
                done(dve, u_log, t, j)
                dve.tensor_reduce(r4[:, 0], L[:, j], AX_X, ALU.max).then_inc(u_max, 1)

            def logits_less_max(t, j):
                done(dve, u_max, t, j)
                dve.tensor_tensor(L[:, j], L[:, j], r4[:, 0].unsqueeze(2).to_broadcast([P, TG, M]),
                                  ALU.subtract).then_inc(u_L, 1)

            def exp_sums(t, j):
                done(dve, u_EX, t, j)
                dve.tensor_reduce(r4[:, 1], EX[:, j], AX_X, ALU.add).then_inc(u_sum, 1)

            def edge_weights(t, j):
                done(dve, u_sum, t, j)
                dve.reciprocal(r4[:, 2], r4[:, 1]).then_inc(u_rec, 1)

            def edge_scales(t, j):
                done(dve, u_rec, t, j)
                dve.tensor_tensor(r4[:, 3], r4[:, 2], wgt[:, bass.ds((RB * t + j) * TG, TG)],
                                  ALU.mult).then_inc(u_scale, 1)

            def head_weights(t, j):
                done(dve, u_scale, t, j)
                dve.tensor_tensor(EX[:, j], EX[:, j], r4[:, 3].unsqueeze(2).to_broadcast([P, TG, M]),
                                  ALU.mult).then_inc(u_head, 1)

            def tile_window(t, j):
                done(dve, u_Q, t, j, RB)
                dve.tensor_tensor(OH[:, j], iota_g[:, 0:WT].unsqueeze(1).to_broadcast([P, TG, WT]),
                                  rel_t[:, bass.ds((RB * t + j) * TG, TG)].unsqueeze(2).to_broadcast([P, TG, WT]),
                                  ALU.is_equal).then_inc(u_OH, 1)

            def window_weights(t, j):
                done(dve, u_head, t, j)
                done(dve, u_OH, t, j)
                done(dve, u_R, t, j, RB)
                dve.tensor_tensor(Q[:, j], OH[:, j].unsqueeze(3).to_broadcast([P, TG, WT, M]),
                                  EX[:, j].unsqueeze(2).to_broadcast([P, TG, WT, M]), ALU.mult).then_inc(u_Q, 1)

            def body1w(t, j):
                back(exp_sums, t, j, 3)
                back(block_mask, t, j, 1)
                back(window1_t, t, j, 0)
                back(logits_less_max, t, j, 2)
                back(edge_weights, t, j, 3)
                back(choose, t, j, 1)
                back(edge_scales, t, j, 3)
                back(tile_window, t, j, 3)
                back(source_logits, t, j, 1)
                back(head_weights, t, j, 3)
                back(sources_t, t, j, 0)
                back(logits, t, j, 1)
                back(window_weights, t, j, 3)
                back(logits_max, t, j, 1)

            flag_ = load_flag(dve)
            with dve.If(flag_):
                over_groups(dve, body1w)
            with dve.Else():
                with dve.Fori(0, PAIRS) as i:
                    group1(i, 0)
                    group1(i, 1)
                group1(PAIRS, 0)

            done_dve(dve, "xb")
            for half, (b0, b1) in OUT_HALVES:
                dve.wait_ge(sums1_in[half], 16 * TG)
                hs = h[:, b0:b1, :]
                step(dve.tensor_tensor(hs, sm[:, 0, b0:b1, 0:D], sm[:, 1, b0:b1, 0:D], ALU.add))
                done_dve(dve, ("y01", half))
                step(dve.tensor_tensor(hs, hs, sm[:, 2, b0:b1, 0:D], ALU.add))
                done_dve(dve, ("y012", half))
                step(dve.tensor_tensor(hs, hs, x[:, b0:b1, :], ALU.add))

        @block.tensor
        def _(pe):
            def turn_nodes(name, chunks):
                for c in chunks:
                    if c >= 2:
                        done_act(pe, (name, c - 2))
                    for n, b in enumerate(chunk_blocks(c)):
                        last = pe.transpose(bank[c % 2][0:D, n * P:(n + 1) * P], h[:, b, :], ident[0:P, 0:P])
                    last.then_inc(pe_step, 1)

            pe.wait_ge(const_ready, 2)
            done_dve(pe, "rawf")
            for k in range(6):
                what, half = k // 2, k % 2
                for n, c in enumerate(range(0, 6) if half == 0 else range(6, NIC)):
                    last = pe.transpose(bank[2 + k][0:P, n * IC:(n + 1) * IC], raw[:, what, c, :], ident[0:IC, 0:IC])
                last.then_inc(pe_step, 1)

            done_dve(pe, ("relu", ""))
            turn_nodes("hT", range(NCH))
            done_dve(pe, ("turned_f", 5))
            pe.wait_ge(win_dve, 1)
            for k in range(2):
                lo, hi = (0, 6 * IC) if k == 0 else (6 * IC, NT)
                pe.matmul(bank[2 + k][0:P, 0:hi - lo], ones[:], dst_f[0:1, lo:hi], start=True, stop=True
                          ).then_inc(win_pe, 1)
            pe.wait_ge(const_ready, CONSTS)
            pe.wait_ge(weights_in, 16 * WL)
            done_act(pe, ("hT", NCH - 1))
            for c in range(NCH):
                if c >= 2:
                    done_act(pe, ("ab", c - 2))
                for n, b in enumerate(chunk_blocks(c)):
                    last = pe.matmul(bank[c % 2][0:P, n * 2 * D:(n + 1) * 2 * D], hT[:, b * P:(b + 1) * P], w_ab[:],
                                     start=True, stop=True)
                last.then_inc(pe_step, 1)
            pe.transpose(bank[5][0:D, 0:DC], w3[:], ident[0:DC, 0:DC]).then_inc(pe_step, 1)
            done_act(pe, "w3T")
            pe.matmul(bank[6][0:DC, 0:D], XT[0:D, 0, 0:DC], wn1a[:], start=True, stop=True).then_inc(pe_step, 1)

            pe.wait_ge(win_dve, WIN_SPAN)
            pe.transpose(bank[4][0:1, 0:P], span[:, 0:1], ident[0:P, 0:P]).then_inc(win_pe, 1)

            done_act(pe, "w3n")

            pe.sem_inc(pe_g[0], 2 * PE0)
            pe.sem_inc(pe_g[1], 2 * PE1)

            def group0(i, j):
                g = 2 * i + j
                pe.wait_ge(rows_in[0][j], (i + 1) * 32)
                pe.wait_ge(dve_g[0], (g + 2) * DVE0 + D0_SUM)
                for q in range(TG):
                    last = pe.transpose(bank[j % 2][:, q * P:(q + 1) * P], X[0:P, j, q, :], ident[0:P, 0:P])
                last.then_inc(pe_g[0], 1)
                pe.wait_ge(act_g[0], (g + 2) * ACT0 + A0_XT)
                pe.matmul(bank[2 + j % 2][0:D, 0:GE], w_ex[:], XT[:, j, :], start=True, stop=True).then_inc(pe_g[0], 1)
                pe.wait_ge(act_g[0], (g + 2) * ACT0 + A0_H1)
                for q in range(TG):
                    last = pe.matmul(bank[4 + j % 2][0:P, q * D:(q + 1) * D], H1[:, j, q * P:(q + 1) * P], w2[:],
                                     start=True, stop=True)
                last.then_inc(pe_g[0], 1)
                pe.wait_ge(act_g[0], (g + 2) * ACT0 + A0_H2)
                for q in range(TG):
                    last = pe.matmul(bank[6 + j % 2][0:P, q * DC:(q + 1) * DC], S[:, j, q, :], H2[:, j, q, :],
                                     start=True, stop=True)
                last.then_inc(pe_g[0], 1)

            def turn_w(t, j):
                pe.wait_ge(x_load[j], (t + 1) * 16)
                for q in range(TG):
                    pe.wait_ge(gat_a[0][j][q], (t + 1) * 16)
                done(pe, f_XT, t, j, 2)
                for q in range(TG):
                    last = pe.transpose(bank[j % 2][:, q * P:(q + 1) * P], X[0:P, j, q, :], ident[0:P, 0:P])
                last.then_inc(f_T, 1)

            def layer1_w(t, j):
                done(pe, f_OT, t, j)
                pe.wait_ge(bw_load[j], (t + 1) * 16)
                done(pe, f_XT, t, j)
                done(pe, f_H1, t, j, 2)
                pe.matmul(bank[2 + j % 2][0:D, 0:GE], w_ex[:], XT[:, j, :], start=True, stop=False)
                pe.matmul(bank[2 + j % 2][0:D, 0:GE], BW[:, j, :], OT[:, j, :], start=False, stop=True
                          ).then_inc(f_h1, 1)

            def layer2_w(t, j):
                done(pe, f_H1, t, j)
                done(pe, f_H2, t, j, 2)
                for q in range(TG):
                    last = pe.matmul(bank[4 + j % 2][0:P, q * D:(q + 1) * D], H1[:, j, q * P:(q + 1) * P], w2[:],
                                     start=True, stop=True)
                last.then_inc(f_h2, 1)

            def segment_w(t, j):
                done(pe, f_H2, t, j)
                done(pe, f_OE, t, j)
                done(pe, f_acc, t, j, 2)
                for q in range(TG):
                    last = pe.matmul(bank[6 + j % 2][0:DC, 0:WG], H2[:, j, q, :], OE[:, j, q, :],
                                     start=(q == 0), stop=(q == TG - 1))
                last.then_inc(f_seg, 1)

            def body0w(t, j):
                back(turn_w, t, j, 0)
                back(layer1_w, t, j, 1)
                back(layer2_w, t, j, 2)
                back(segment_w, t, j, 3)

            flag_ = load_flag(pe)
            with pe.If(flag_):
                over_groups(pe, body0w)
            with pe.Else():
                with pe.Fori(0, PAIRS) as i:
                    group0(i, 0)
                    group0(i, 1)
                group0(PAIRS, 0)
                pe.wait_ge(sum_dve, 2)
                for c in range(NCH):
                    if c >= 2:
                        pe.wait_ge(sum_act, c - 1)
                    for n, b in enumerate(chunk_blocks(c)):
                        last = pe.transpose(bank[c % 2][0:DC, n * P:(n + 1) * P], sm[:, 0, b, :], ident[0:P, 0:P])
                    last.then_inc(sum_pe, 1)

            pe.wait_ge(sT_ready, 1)
            for k in range(NCH + 2):
                if k < NCH:
                    c, (lo, hi) = k, chunk_cols(k)
                    if c >= 2:
                        done_act(pe, ("g1", c - 2))
                    pe.matmul(bank[c % 2][0:D, 0:hi - lo], wn1h[:], hT[:, lo:hi], start=True, stop=False)
                    pe.matmul(bank[c % 2][0:D, 0:hi - lo], w3[:], sT[:, lo:hi], start=False, stop=True
                              ).then_inc(pe_step, 1)
                if 1 <= k <= NCH:
                    c, (lo, hi) = k - 1, chunk_cols(k - 1)
                    done_act(pe, ("g1", c))
                    if c >= 2:
                        done_act(pe, ("g2", c - 2))
                    pe.matmul(bank[2 + c % 2][0:D, 0:hi - lo], wn2[:], hT[:, lo:hi], start=True, stop=True
                              ).then_inc(pe_step, 1)
                if k >= 2:
                    c = k - 2
                    done_act(pe, ("g2", c))
                    if c >= 2:
                        done_dve(pe, ("x1", c - 2))
                    for n, b in enumerate(chunk_blocks(c)):
                        last = pe.matmul(bank[4 + c % 2][0:P, n * D:(n + 1) * D], nT2[:, b * P:(b + 1) * P], wn3[:],
                                         start=True, stop=True)
                    last.then_inc(pe_step, 1)

            for half, chunks in HALVES:
                done_dve(pe, ("relu", half))
                turn_nodes("h'T", chunks)
                done_act(pe, ("h'T", chunks[-1]))
                for b in range(*blocks_in(chunks)):
                    last = pe.matmul(bank[6][0:P, b * 2 * M:(b + 1) * 2 * M], hT[:, b * P:(b + 1) * P], w_u[:],
                                     start=True, stop=True)
                last.then_inc(pe_step, 1)
                for b in Z_BLOCKS[half]:
                    if b >= 2:
                        done_act(pe, ("z", b - 2))
                    pe.matmul(bank[2 + b % 2][0:P, :], hT[0:D, b * P:(b + 1) * P],
                              w_z[:].rearrange("c m d -> c (m d)"), start=True, stop=True).then_inc(pe_step, 1)
            done_act(pe, ("z", NB - 1))

            def group1(i, j):
                g = 2 * i + j
                pe.wait_ge(dve_g[1], (g + 2) * DVE1 + D1_Z)
                for q in range(TG):
                    for m in range(M):
                        last = pe.matmul(bank[6 + j % 2][0:P, q * D:(q + 1) * D], S[:, j, q, :],
                                         Z[:, j, q, m * D:(m + 1) * D], start=(m == 0), stop=(m == M - 1))
                last.then_inc(pe_g[1], 1)

            def logits_w(t, j):
                done(pe, u_OT, t, j)
                pe.wait_ge(bw_load[j], (NG - j + RB - 1) // RB * 16 + (t + 1) * 16)
                done(pe, u_log, t, j, 1)
                for q in range(TG):
                    for k in range(PARTS):
                        last = pe.matmul(bank[4][0:P, q * M:(q + 1) * M], OT1[:, j, q * P:(q + 1) * P],
                                         VW[:, j, k, :], start=(k == 0), stop=(k == PARTS - 1))
                last.then_inc(u_V, 1)

            def candidates_w(t, j):
                done(pe, u_OLT, t, j)
                done(pe, u_TM, t, j, 2)
                for q in range(TG):
                    for k in range(PARTS):
                        last = pe.matmul(pair[3 * (j % 2)][0:P, q * TW:q * TW + NB * M],
                                         OLT[:, j, q * P:(q + 1) * P], u_parts[:, k, :],
                                         start=(k == 0), stop=(k == PARTS - 1))
                last.then_inc(u_cand, 1)

            def reduce_w(t, j):
                done(pe, u_Q, t, j)
                done(pe, u_S, t, j)
                for q in range(TG):
                    last = pe.matmul(bank[2 + j % 2][:, q * P:(q + 1) * P], Q[:, j, q].rearrange("p n m -> p (n m)"),
                                     S[:, j, q, :], start=True, stop=True)
                last.then_inc(u_R, 1)

            def combine_w(t, j):
                done(pe, u_RS, t, j)
                pe.wait_ge(zw_load[j], (t + 1) * 16 * TG)
                done(pe, u_CS, t, j, 1)
                for q in range(TG):
                    last = pe.matmul(bank[5][0:P, q * D:(q + 1) * D], R[:, j, q * P:(q + 1) * P],
                                     ZW[:, j, q, :], start=True, stop=True)
                last.then_inc(u_C, 1)

            def body1w(t, j):
                back(logits_w, t, j, 1)
                back(reduce_w, t, j, 4)
                back(combine_w, t, j, 5)
                back(candidates_w, t, j, 0)

            flag_ = load_flag(pe)
            with pe.If(flag_):
                done_dve(pe, "u3")
                over_groups(pe, body1w)
            with pe.Else():
                with pe.Fori(0, PAIRS) as i:
                    group1(i, 0)
                    group1(i, 1)
                group1(PAIRS, 0)


NAMES = ["x", "src", "dst", "edge_attr_64", "edge_weight", "L0_gnn_We1", "L0_gnn_be1", "L0_gnn_We2", "L0_gnn_be2",
         "L0_gnn_We3", "L0_gnn_be3", "L0_gnn_Wn1", "L0_gnn_bn1", "L0_gnn_Wn2", "L0_gnn_bn2", "L0_gnn_Wn3",
         "L0_gnn_bn3", "L1_gnn_var_u", "L1_gnn_var_c", "L1_gnn_var_w", "L1_gnn_var_b"]


def kernel(**inputs):
    import numpy as _np
    import concourse.bacc as _bacc
    from concourse import mybir as _mybir
    from concourse.bass_utils import run_bass_kernel_spmd as _run

    nc = _bacc.Bacc("TRN2", target_bir_lowering=False, num_devices=1)
    arrays, aps = {}, {}
    for name in NAMES:
        v = _np.ascontiguousarray(inputs[name])
        arrays[f"in_{name}"] = v
        aps[name] = nc.dram_tensor(f"in_{name}", v.shape, _mybir.dt.from_np(v.dtype), kind="ExternalInput").ap()
    out = nc.dram_tensor("out_0", (N, D), _mybir.dt.float32, kind="ExternalOutput").ap()
    build_gnn(nc, aps, out)
    r = _run(nc, [arrays], core_ids=[0])
    return r.results[0]["out_0"]
```
